# Optimizing a Trainium2 kernel written in Bass

```python
import numpy as np
import jax
import jax.numpy as jnp

def _softmax(x, axis=-1):
    return jax.nn.softmax(x, axis=axis)

def _gelu(x):
    return jax.nn.gelu(x, approximate=True)

def _silu(x):
    return jax.nn.silu(x)

def _sigmoid(x):
    return jax.nn.sigmoid(x)

def _layernorm(x, axis=-1, eps=1e-05):
    m = jnp.mean(x, axis=axis, keepdims=True)
    v = jnp.var(x, axis=axis, keepdims=True)
    return (x - m) / jnp.sqrt(v + eps)

def _scatter_add(tgt, idx, src, axis=0):
    return tgt.at[idx].add(src)

def _segment_sum(src, seg, n):
    return jax.ops.segment_sum(src, seg, n)
kernel_name = 'mk_early_fusion_d1_tok_img1024_r4_65bcc5'

def setup_inputs(seed: int=0):
    np.random.seed(seed)
    _w = jnp.asarray

    def _rec_inputs():
        import jax
        import jax.numpy as jnp
        _rk = jax.random.key(seed)
        x = 0.00021031 + 1.00007 * jax.random.normal(jax.random.fold_in(_rk, 1), (32, 1, 256, 256), jnp.float32)
        txt = 0.949517 + 0.151997 * jax.random.normal(jax.random.fold_in(_rk, 2), (32, 77, 256), jnp.float32)
        return (x, txt)
    x, txt = _rec_inputs()

    def _L0_tok_setup():
        import jax, jax.numpy as jnp
        import numpy as np
        KERNEL = jnp.array([[[[1.0, 0.0], [0.0, -1.0]]], [[[0.0, -1.0], [1.0, 0.0]]]], dtype=jnp.float32)
        key = jax.random.key(seed)
        images = jax.random.normal(key, (32, 1, 256, 256), dtype=jnp.float32)
        return {'images': images}
    _L0_tok_all = _L0_tok_setup()
    _L0_tok_in = {k: v for k, v in _L0_tok_all.items() if k in ()}
    del _L0_tok_all

    def _L0_attn_setup():
        import jax, jax.numpy as jnp
        import numpy as np
        import math
        EMBED_DIM = 256
        NUM_HEADS = 16
        HEAD_DIM = EMBED_DIM // NUM_HEADS
        key = jax.random.key(seed)
        ks = jax.random.split(key, 5)
        B, S, D = (2, 512, EMBED_DIM)
        s = 1.0 / math.sqrt(D)
        x = jax.random.normal(ks[0], (B, S, D), dtype=jnp.float32)
        W_qkv = jax.random.normal(ks[1], (3 * D, D), dtype=jnp.float32) * s
        b_qkv = jax.random.normal(ks[2], (3 * D,), dtype=jnp.float32) * 0.01
        W_out = jax.random.normal(ks[3], (D, D), dtype=jnp.float32) * s
        b_out = jax.random.normal(ks[4], (D,), dtype=jnp.float32) * 0.01
        return {'x': x, 'W_qkv': W_qkv, 'b_qkv': b_qkv, 'W_out': W_out, 'b_out': b_out}
    _L0_attn_all = _L0_attn_setup()
    _L0_attn_in = {k: v for k, v in _L0_attn_all.items() if k in ('W_qkv', 'b_qkv', 'W_out', 'b_out')}
    del _L0_attn_all

    def _L0_ffn_setup():
        import jax, jax.numpy as jnp
        import numpy as np

        def _bitlinear(x, w_latent):
            scale = jax.lax.stop_gradient(jnp.clip(jnp.mean(jnp.abs(w_latent), axis=1, keepdims=True), 1e-05, None))
            tern = jnp.clip(jnp.round(w_latent / scale), -1.0, 1.0)
            w = w_latent + jax.lax.stop_gradient(tern - w_latent)
            return x @ (w * scale).T
        key = jax.random.key(seed)
        ks = jax.random.split(key, 6)
        dim, hidden, rank = (256, 1024, 16)
        B, S = (4, 1024)
        x = jax.random.normal(ks[0], (B, S, dim), dtype=jnp.float32)
        w_fc = 0.02 * jax.random.normal(ks[1], (hidden, dim), dtype=jnp.float32)
        w_proj = 0.02 * jax.random.normal(ks[2], (dim, hidden), dtype=jnp.float32)
        u = 0.02 * jax.random.normal(ks[3], (hidden, rank), dtype=jnp.float32)
        v = 0.02 * jax.random.normal(ks[4], (rank, dim), dtype=jnp.float32)
        fast_b = jax.random.normal(ks[5], (rank, rank), dtype=jnp.float32)
        gate = jnp.float32(0.05)
        return {'x': x, 'fast_b': fast_b, 'w_fc': w_fc, 'w_proj': w_proj, 'u': u, 'v': v, 'gate': gate}
    _L0_ffn_all = _L0_ffn_setup()
    _L0_ffn_in = {k: v for k, v in _L0_ffn_all.items() if k in ('fast_b', 'w_fc', 'w_proj', 'u', 'v', 'gate')}
    del _L0_ffn_all
    return {'x': x, 'txt': txt, 'L0_attn_W_qkv': _L0_attn_in['W_qkv'], 'L0_attn_b_qkv': _L0_attn_in['b_qkv'], 'L0_attn_W_out': _L0_attn_in['W_out'], 'L0_attn_b_out': _L0_attn_in['b_out'], 'L0_ffn_fast_b': _L0_ffn_in['fast_b'], 'L0_ffn_w_fc': _L0_ffn_in['w_fc'], 'L0_ffn_w_proj': _L0_ffn_in['w_proj'], 'L0_ffn_u': _L0_ffn_in['u'], 'L0_ffn_v': _L0_ffn_in['v'], 'L0_ffn_gate': _L0_ffn_in['gate']}

def reference(x, txt, L0_attn_W_qkv, L0_attn_b_qkv, L0_attn_W_out, L0_attn_b_out, L0_ffn_fast_b, L0_ffn_w_fc, L0_ffn_w_proj, L0_ffn_u, L0_ffn_v, L0_ffn_gate):
    import jax
    import jax.numpy as jnp

    def _L0_tok_ref(images):
        import jax, jax.numpy as jnp
        import numpy as np
        KERNEL = jnp.array([[[[1.0, 0.0], [0.0, -1.0]]], [[[0.0, -1.0], [1.0, 0.0]]]], dtype=jnp.float32)
        out = jax.lax.conv_general_dilated(images, KERNEL, window_strides=(1, 1), padding=((0, 1), (0, 1)), dimension_numbers=('NCHW', 'OIHW', 'NCHW'))
        return jnp.clip(jnp.sum(jnp.abs(out), axis=1), 0.0, 1.0)

    def _L0_attn_ref(x, W_qkv, b_qkv, W_out, b_out):
        import jax, jax.numpy as jnp
        import numpy as np
        import math
        EMBED_DIM = 256
        NUM_HEADS = 16
        HEAD_DIM = EMBED_DIM // NUM_HEADS
        B, S, D = x.shape
        H, Hd = (NUM_HEADS, HEAD_DIM)
        slopes = jnp.power(2.0, 8.0 * jnp.arange(0, -H, -1, dtype=jnp.float32) / H)
        qkv = x @ W_qkv.T + b_qkv
        qkv = qkv.reshape(B, S, 3, H, Hd).transpose(2, 0, 3, 1, 4)
        q, k, v = (qkv[0], qkv[1], qkv[2])
        scores = jnp.einsum('bhqd,bhkd->bhqk', q, k) / math.sqrt(Hd)
        pos = jnp.arange(S)
        rel = jnp.abs(pos[None, :] - pos[:, None]).astype(jnp.float32)
        bias = -slopes[:, None, None] * rel
        probs = jax.nn.softmax(scores + bias[None], axis=-1)
        out = jnp.einsum('bhqk,bhkd->bhqd', probs, v)
        out = out.transpose(0, 2, 1, 3).reshape(B, S, D)
        return out @ W_out.T + b_out

    def _L0_ffn_ref(x, fast_b, w_fc, w_proj, u, v, gate):
        import jax, jax.numpy as jnp
        import numpy as np

        def _bitlinear(x, w_latent):
            scale = jax.lax.stop_gradient(jnp.clip(jnp.mean(jnp.abs(w_latent), axis=1, keepdims=True), 1e-05, None))
            tern = jnp.clip(jnp.round(w_latent / scale), -1.0, 1.0)
            w = w_latent + jax.lax.stop_gradient(tern - w_latent)
            return x @ (w * scale).T
        h = _bitlinear(x, w_fc) + gate * (x @ v.T @ fast_b.T @ u.T)
        r = jnp.maximum(h, 0.0)
        return _bitlinear(r * r, w_proj)
    h = _L0_tok_ref(x)
    h = jnp.concatenate([h, txt], axis=1)
    h = h + _L0_attn_ref(_layernorm(h, axis=-1), L0_attn_W_qkv, L0_attn_b_qkv, L0_attn_W_out, L0_attn_b_out)
    h = h + _L0_ffn_ref(_layernorm(h, axis=-1), L0_ffn_fast_b, L0_ffn_w_fc, L0_ffn_w_proj, L0_ffn_u, L0_ffn_v, L0_ffn_gate)
    return h

_drawn_inputs = setup_inputs


def setup_inputs(seed=0):
    import zlib

    import numpy as np

    out = dict(_drawn_inputs(seed))
    spreads = {}
    factors = {'L0_attn_b_qkv': 4.742,
     'L0_attn_b_out': 5.863,
     'L0_ffn_fast_b': 8.0,
     'L0_ffn_u': 8.0,
     'L0_ffn_v': 8.0}
    for name, (base, spread) in spreads.items():
        noise = np.random.default_rng([zlib.crc32(name.encode()), seed]).standard_normal(out[name].shape)
        drawn = base * np.exp(spread * noise) if base else spread * noise
        out[name] = jnp.asarray(drawn.astype(out[name].dtype))
    for name, factor in factors.items():
        out[name] = (out[name] * factor).astype(out[name].dtype)
    return out
```

```python
from contextlib import ExitStack

import numpy as np

import concourse.bass as bass
from concourse import mybir

F32 = mybir.dt.float32
BF16 = mybir.dt.bfloat16
I32 = mybir.dt.int32
ALU = mybir.AluOpType
ACT = mybir.ActivationFunctionType
AX = mybir.AxisListType

B, IMG, TXT, D = 32, 256, 77, 256
S = IMG + TXT
P = 128
ROWS = [P, P, S - 2 * P]
NT = len(ROWS)
SP3 = NT * P
H, HD = 16, 16
HID, RANK = 1024, 16
NC = D // P
NM = HID // P
HALF = H // 2
EPS = 1e-5
Q_PARTS = [0, 0, 1, 1, 0, 2]
K_PARTS = [0, 1, 0, 1, 2, 0]
KAUG = HD * len(Q_PARTS)
RING = 8
NQ = 2 * NC
BW = S + 2 * P

USES = [
    ("otok2", 0, "prev"),
    ("otok3", 1, "prev"), ("v0", 2, "own"), ("v1", 0, "own"), ("v2", 1, "own"),
    ("xt0", 2, "next"), ("xt1", 0, "next"), ("ont0", 1, "prev"), ("ont1", 2, "prev"),
    ("qk0", 0, "next"), ("qk1", 1, "next"), ("proj0", 2, "prev"), ("proj1", 0, "prev"),
    ("qk2", 1, "next"), ("qk3", 2, "next"),
    ("otok0", 0, "own"), ("x2t0", 1, "prev"), ("x2t1", 2, "prev"),
    ("ffn0", 0, "prev"), ("ffn1", 1, "prev"), ("ffn2", 2, "prev"), ("ffn3", 0, "prev"),
    ("ffn4", 1, "prev"), ("ffn5", 2, "prev"),
    ("otok1", 0, "own"), ("ffn6", 1, "prev"), ("ffn7", 2, "prev"),
    ("y0", 0, "prev"), ("y1", 1, "prev"), ("y2", 2, "prev"),
]
BANK_OF = {name: bank for name, bank, _ in USES}
SETUP_BANKS = [((n + 1) % 3, (n + 1) // 3) for n in range(8)]
SETUP_USES = [3, 3, 3]


def parts_of(it):
    if not isinstance(it, int):
        return ("own", "prev", "next")
    return tuple(p for p, on in (("own", 0 <= it < B), ("prev", it > 0), ("next", it < B - 1)) if on)


def uses_in(bank, parts, before=None):
    n = 0
    for name, k, part in USES:
        if name == before:
            break
        n += k == bank and part in parts
    return n


def bank_uses_before(name, it):
    k = BANK_OF[name]
    n = SETUP_USES[k] + uses_in(k, parts_of(it), before=name)
    if isinstance(it, int) and it == -1:
        return n
    n += uses_in(k, ("next",))
    if isinstance(it, int) and it == 0:
        return n
    n += uses_in(k, ("own", "next"))
    every = uses_in(k, ("own", "prev", "next"))
    if isinstance(it, int) and it == B:
        return n + every * (B - 2) + uses_in(k, ("own", "prev"))
    return (it - 1) * every + n


def early_fusion_kernel(nc, x, txt, wqkvT, bqk, bv, woT, bo, fast_bT, w_fc, w_proj, uT, v, gate, out):
    ctx = ExitStack()
    with ctx:
        def sb(name, shape, dt=F32):
            return ctx.enter_context(nc.sbuf_tensor(name, shape, dt))

        def psum(name):
            return ctx.enter_context(nc.psum_tensor(name, [P, 512], F32))

        def sem(name):
            return ctx.enter_context(nc.semaphore(name))

        wqkv_sb = sb("wqkv_sb", [P, NC, 3 * D])
        wo_sb = sb("wo_sb", [P, NC, D])
        w1T = sb("w1T", [P, NC, HID])
        w2T = sb("w2T", [P, NM, D])
        bqk_sb = sb("bqk_sb", [P, NQ])
        bias_bc = sb("bias_bc", [P, 2, D])
        ident = sb("ident", [P, P])
        dist = sb("dist", [P, H, BW])
        mhalf = sb("mhalf", [P, NT])

        imgA = sb("imgA", [P, 2, IMG + 1])
        imgB = sb("imgB", [P, 2, IMG + 1])
        edges = sb("edges", [P, 2, 2, IMG])
        h_new = sb("h_new", [P, NT, D])
        h_bias = sb("h_bias", [P, NT, D])
        h_old = sb("h_old", [P, NT, D])
        stats = sb("stats", [P, 2, NT, 6])
        moments = sb("moments", [P, 2, NT, 2])
        var_eps = sb("var_eps", [P, 2, NT])
        rstd = sb("rstd", [P, 2, NT])
        xn = sb("xn", [P, NT, D])
        xT = sb("xT", [P, NC, SP3])
        qk = sb("qk", [P, NQ, S])
        rest = sb("rest", [P, NQ, S])
        qk_parts = sb("qk_parts", [P, 3, NQ, S], BF16)
        q_aug = sb("q_aug", [KAUG, H, S], BF16)
        k_aug = sb("k_aug", [KAUG, H, S], BF16)

        v_sb = sb("v_sb", [P, NT, H, 32])
        nscore = sb("nscore", [P, 2, NT, S])
        nmax = sb("nmax", [P, 2, NT])
        probs = sb("probs", [P, 2, NT, S])
        probsT = sb("probsT", [P, RING, NT, S])
        oT = sb("oT", [P, SP3])
        recip = sb("recip", [P, NT, 4])
        o_norm = sb("o_norm", [P, NT, D])

        o_normT = sb("o_normT", [P, NC, SP3])
        h_mid = sb("h_mid", [P, NT, D])
        x2 = sb("x2", [P, NT, D])
        x2T = sb("x2T", [P, NC, SP3])
        act_T = sb("act_T", [P, NM, S])
        y_sb = x2

        flat = probsT[:, :, :, :].rearrange("p r t s -> p (r t s)")
        w1_nat = flat[:, 0:NM * D].rearrange("p (m d) -> p m d", m=NM)
        w2_nat = flat[:, NM * D:2 * NM * D].rearrange("p (c m) -> p c m", c=NC)
        t_pos = flat[:, 2 * NM * D:3 * NM * D]
        t_neg = act_T[:, :, :].rearrange("p m s -> p (m s)")[:, 0:NM * D]
        dist_i = nscore[:, :, :, :].rearrange("p r t s -> p (r t s)")[:, 0:BW].bitcast(I32)
        dist_f = nscore[:, :, :, :].rearrange("p r t s -> p (r t s)")[:, BW:2 * BW]
        low_uT = probs[0:RANK, :, :, :].rearrange("p r t s -> p (r t s)")[:, 0:HID]
        low_v = xn[0:RANK, 0, :]
        low_bT = xn[0:RANK, 1, 0:RANK]
        low_bv = xn[0:RANK, 2, :]
        gate_bc = xT[:, 0, 0:1]
        bias_row = y_sb[0:1, :, :].rearrange("p t d -> p (t d)")[:, 0:2 * D + 1]
        scale1 = sb("scale1", [P, NM])
        half1 = sb("half1", [P, 2, NM])
        scale2 = sb("scale2", [P, NC])
        half2 = sb("half2", [P, 2, NC])

        score_ps = [psum("score_ps0"), psum("score_ps1")]
        turn_ps = [psum("turn_ps0"), psum("turn_ps1")]
        o_ps = psum("o_ps")
        bank = [psum("bank0"), psum("bank1"), psum("bank2")]

        waits_met = sem("waits_met")
        weights_loaded = sem("weights_loaded")
        pool_step = sem("pool_step")
        consts_ready = sem("consts_ready")
        rows_ready = sem("rows_ready")
        dve_step = sem("dve_step")
        low_filled = sem("low_filled")
        low_ready = sem("low_ready")
        bias_scaled = sem("bias_scaled")
        filled = [sem(f"bank_filled{k}") for k in range(3)]
        drained = [sem(f"bank_drained{k}") for k in range(3)]
        tokens_loaded = sem("tokens_loaded")
        edges_ready = sem("edges_ready")
        edges_abs = sem("edges_abs")
        edges_sum = sem("edges_sum")
        tokens_ready = sem("tokens_ready")
        stats_done = [sem("stats1_done"), sem("stats2_done")]
        moments_done = [sem("moments1_done"), sem("moments2_done")]
        eps_added = [sem("eps1_added"), sem("eps2_added")]
        rstd_ready = [sem("rstd1_ready"), sem("rstd2_ready")]
        xn_ready = sem("xn_ready")
        x2_ready = sem("x2_ready")
        h_bias_ready = sem("h_bias_ready")
        h_old_loaded = sem("h_old_loaded")
        high_ready = sem("high_ready")
        rest_ready = sem("rest_ready")
        middle_ready = sem("middle_ready")
        low_part_ready = sem("low_part_ready")
        aug_loaded = [sem("aug_loaded0"), sem("aug_loaded1")]
        scores_ready = sem("scores_ready")
        scores_taken = sem("scores_taken")
        probs_ready = sem("probs_ready")
        turned = [sem("turned0"), sem("turned1")]
        turned_taken = [sem("turned_taken0"), sem("turned_taken1")]
        o_ready = sem("o_ready")
        o_taken = sem("o_taken")
        recip_ready = sem("recip_ready")
        squares_ready = sem("squares_ready")
        stored = sem("stored")

        def fill_wait(eng, name, it):
            n = bank_uses_before(name, it)
            if not (isinstance(n, int) and n == 0):
                eng.wait_ge(drained[BANK_OF[name]], n)

        def take_wait(eng, name, it):
            eng.wait_ge(filled[BANK_OF[name]], bank_uses_before(name, it) + 1)

        def wait_alone(eng, semaphore, value):
            eng.wait_ge(semaphore, value)
            if not isinstance(value, int):
                eng.sem_inc(waits_met, 1)

        def step_taken(eng, name, it):
            wait_alone(eng, drained[BANK_OF[name]], bank_uses_before(name, it) + 1)

        def rows(t):
            return ROWS[t]

        def lagged(b, s, lag):
            if s >= lag:
                return b, s - lag
            if isinstance(b, int) and b == 0:
                return None
            return b - 1, s - lag + H

        def turn(b, h, u):
            m = NT * h + u
            return m % 2, b * (NT * H // 2) + m // 2 + 1

        def iterations(eng, body):
            body(-1)
            body(0)
            with eng.Fori(1, B - 1) as b:
                body(b)
            body(B - 1)
            body(B)

        def has(part, it):
            return part in parts_of(it)

        block = ctx.enter_context(nc.Block())

        @block.sync
        def _(sp):
            loads = [
                (wqkv_sb[:, :, :], wqkvT.rearrange("(c p) n -> p c n", p=P)),
                (wo_sb[:, :, :], woT.rearrange("(c p) n -> p c n", p=P)),
                (bqk_sb[:, :], bqk),
                (w1_nat, w_fc.rearrange("(m p) d -> p m d", p=P)),
                (w2_nat, w_proj.rearrange("(c p) m -> p c m", p=P)),
                (low_uT, uT), (low_v, v), (low_bT, fast_bT),
                (bias_row[:, 0:D], bv), (bias_row[:, D:2 * D], bo), (bias_row[:, 2 * D:2 * D + 1], gate),
            ]
            sp.sem_inc(stored, 32)
            for dst, src in loads:
                sp.dma_start(dst, src).then_inc(weights_loaded, 16)
            sp.wait_ge(consts_ready, 1)

            def load_tokens(n):
                img = x[n, 0]
                sp.dma_start(imgA[:, :, 0:IMG], img.rearrange("(t p) c -> p t c", p=P)).then_inc(tokens_loaded, 16)
                sp.dma_start(imgB[:, 0, 0:IMG], img[1:P + 1, :]).then_inc(tokens_loaded, 16)
                sp.dma_start(imgB[0:112, 1, 0:IMG], img[P + 1:P + 113, :]).then_inc(tokens_loaded, 16)
                sp.dma_start(imgB[112:127, 1, 0:IMG], img[P + 113:IMG, :]).then_inc(tokens_loaded, 16)
                sp.dma_start(h_new[0:TXT, 2, :], txt[n]).then_inc(tokens_loaded, 16)

            def load_aug(half):
                for aug, parts, block_ in ((q_aug, Q_PARTS, half), (k_aug, K_PARTS, 2 + half)):
                    for i, part in enumerate(parts):
                        sp.dma_start(aug[HD * i:HD * (i + 1), HALF * half:HALF * (half + 1), :],
                                     qk_parts[:, part, block_, :]).then_inc(aug_loaded[half], 16)

            def body(it):
                if has("next", it):
                    if not (isinstance(it, int) and it == -1):
                        wait_alone(sp, xn_ready, it + 1)
                        wait_alone(sp, h_bias_ready, it + 1)
                    load_tokens(it + 1)
                if has("own", it):
                    wait_alone(sp, h_bias_ready, it + 1)
                    if has("prev", it):
                        step_taken(sp, "proj1", it)
                    sp.dma_start(h_old[:, :, :], h_bias[:, :, :]).then_inc(h_old_loaded, 16)
                if has("next", it):
                    wait_alone(sp, low_part_ready, it + 2)
                    if has("own", it):
                        wait_alone(sp, scores_ready, it * (NT * H) + NT * HALF)
                    load_aug(0)
                    if has("own", it):
                        wait_alone(sp, scores_ready, it * (NT * H) + NT * H)
                    load_aug(1)
                if has("prev", it):
                    for t in range(NT):
                        step_taken(sp, f"y{t}", it)
                    sp.dma_start(out[it - 1, 0:2 * P, :].rearrange("(t p) d -> p t d", p=P),
                                 y_sb[:, 0:2, :]).then_inc(stored, 16)
                    sp.dma_start(out[it - 1, 2 * P:S, :], y_sb[0:TXT, 2, :]).then_inc(stored, 16)

            iterations(sp, body)
            sp.wait_ge(stored, 32 * (B + 1))

        @block.gpsimd
        def _(pool):
            pool.memset(imgA[:, :, :], 0.0)
            pool.memset(imgB[:, :, :], 0.0)
            pool.memset(h_new[:, :, :], 0.0)
            pool.memset(oT[:, :], 1.0)
            pool.memset(v_sb[:, :, :, HD:HD + 1], 1.0)
            pool.memset(v_sb[:, :, :, HD + 1:32], 0.0)
            pool.memset(mhalf[:, :], -0.5).then_inc(consts_ready, 1)
            pool.memset(ident[:, :], 0.0).then_inc(pool_step, 1)
            pool.iota(dist_i, pattern=[[1, BW]], base=-2 * P, channel_multiplier=-1).then_inc(pool_step, 1)
            pool.wait_ge(pool_step, 2)
            pool.affine_select(out=ident[:, :], in_=ident[:, :], compare_op=ALU.not_equal, fill=1.0,
                               base=0, pattern=[[-1, P]], channel_multiplier=1).then_inc(consts_ready, 1)
            pool.wait_ge(weights_loaded, 16 * 11)
            pool.partition_broadcast(bias_bc[:, :, :].rearrange("p a d -> p (a d)"), bias_row[:, 0:2 * D],
                                     channels=P).then_inc(rows_ready, 1)
            pool.partition_broadcast(gate_bc, bias_row[:, 2 * D:2 * D + 1], channels=P).then_inc(rows_ready, 1)
            pool.wait_ge(rows_ready, 2)

            def make_rstd(k, n):
                wait_alone(pool, moments_done[k], n + 1)
                pool.tensor_scalar(var_eps[:, k, :], moments[:, k, :, 1], EPS, None, ALU.add).then_inc(eps_added[k], 1)
                pool.wait_ge(eps_added[k], n + 1)
                pool.tensor_tensor(rstd[:, k, :], var_eps[:, k, :], mhalf[:, :], ALU.pow).then_inc(rstd_ready[k], 1)

            def body(it):
                nxt = it + 1
                if has("next", it):
                    pool.wait_ge(tokens_loaded, nxt * 80 + 80)
                    pool.tensor_tensor(edges[:, 0, :, :], imgA[:, :, 0:IMG], imgB[:, :, 1:IMG + 1],
                                       ALU.subtract)
                    pool.tensor_tensor(edges[:, 1, :, :], imgB[:, :, 0:IMG], imgA[:, :, 1:IMG + 1],
                                       ALU.subtract).then_inc(edges_ready, 1)
                    pool.wait_ge(edges_abs, nxt + 1)
                    pool.tensor_tensor(edges[:, 0, :, :], edges[:, 0, :, :], edges[:, 1, :, :],
                                       ALU.add).then_inc(edges_sum, 1)
                    wait_alone(pool, edges_sum, nxt + 1)
                    pool.tensor_scalar(h_new[:, 0:2, :], edges[:, 0, :, :], 0.0, 1.0, ALU.max,
                                       ALU.min).then_inc(tokens_ready, 1)
                    make_rstd(0, nxt)
                if has("prev", it):
                    make_rstd(1, it - 1)
                if has("next", it):
                    pool.wait_ge(high_ready, nxt + 1)
                    pool.tensor_tensor(rest[:, :, :], qk[:, :, :], qk_parts[:, 0, :, :],
                                       ALU.subtract).then_inc(rest_ready, 1)
                    if has("own", it):
                        pool.wait_ge(h_old_loaded, it * 16 + 16)
                    pool.tensor_tensor(h_bias[:, :, :], h_new[:, :, :],
                                       bias_bc[:, 1:2, :].to_broadcast([P, NT, D]),
                                       ALU.add).then_inc(h_bias_ready, 1)
                    pool.wait_ge(middle_ready, nxt + 1)
                    pool.tensor_tensor(qk_parts[:, 2, :, :], rest[:, :, :], qk_parts[:, 1, :, :],
                                       ALU.subtract).then_inc(low_part_ready, 1)
                if has("prev", it):
                    for m in range(0, NM, 2):
                        step_taken(pool, f"ffn{m}", it)
                        step_taken(pool, f"ffn{m + 1}", it)
                        pool.tensor_tensor(act_T[:, m:m + 2, :], act_T[:, m:m + 2, :], act_T[:, m:m + 2, :],
                                           ALU.mult).then_inc(squares_ready, 1)

            iterations(pool, body)

        @block.scalar
        def _(act):
            act.wait_ge(consts_ready, 2)
            act.wait_ge(weights_loaded, 16 * 11)

            def take(name, it, dst, rows_=P, **how):
                take_wait(act, name, it)
                k = BANK_OF[name]
                act.activation(dst, bank[k][0:rows_, 0:dst.shape[-1]], how.pop("func", ACT.Copy),
                               **how).then_inc(drained[k], 1)

            def exps(b, h):
                for t in range(NT):
                    act.wait_ge(scores_taken, b * (NT * H) + NT * h + t + 1)
                    if t == 0 and not (isinstance(b, int) and b == 0 and h < 2):
                        two = lagged(b, h, 2)
                        for u in (1, 2):
                            k, n = turn(*two, u)
                            act.wait_ge(turned[k], n)
                    act.activation(probs[0:rows(t), h % 2, t, :], nscore[0:rows(t), h % 2, t, :], ACT.Exp,
                                   bias=nmax[0:rows(t), h % 2, t:t + 1], scale=-1.0).then_inc(probs_ready, 1)

            def body(it):
                nxt, prv = it + 1, it - 1
                for s in range(H):
                    if (one := lagged(it, s, 1)) and (has("own", it) or (s < 1 and it == B)):
                        exps(*one)
                    if (two := lagged(it, s, 2)) and (has("own", it) or (s < 2 and it == B)):
                        b, h = two
                        if not (isinstance(b, int) and b == 0 and h < RING):
                            act.wait_ge(o_ready, b * 4 + h // 4 - 1)
                        for u in (0, 2):
                            k, n = turn(b, h, u)
                            act.wait_ge(turned[k], n)
                            act.activation(probsT[0:rows(u), h % RING, u, :], turn_ps[k][0:rows(u), 0:S],
                                           ACT.Copy).then_inc(turned_taken[k], 1)
                    if s % 4 == 3 and (got := lagged(it, s, 7)) and (has("own", it) or (s == 3 and it == B)):
                        b, h = got
                        g = h // 4
                        act.wait_ge(o_ready, b * 4 + g + 1)
                        if not (isinstance(b, int) and b == 0 and g == 0):
                            pb, pg = (b, g - 1) if g else (b - 1, 3)
                            take_wait(act, f"otok{pg}", pb + 1 if pg >= 2 else pb)
                        act.activation(oT[:, 0:S], o_ps[:, 0:S], ACT.Copy).then_inc(o_taken, 1)
                    if s == 1 and has("next", it):
                        act.wait_ge(edges_ready, nxt + 1)
                        act.activation(edges[:, :, :, :], edges[:, :, :, :], ACT.Abs).then_inc(edges_abs, 1)
                    if s == 5 and has("next", it):
                        for c in range(NC):
                            take(f"xt{c}", it, xT[:, c, :])
                    if s in (6, 7) and has("next", it):
                        for j in (0, 1) if s == 6 else (2, 3):
                            take(f"qk{j}", it, qk[:, j, :], func=ACT.Identity, bias=bqk_sb[:, j:j + 1],
                                 scale=HD ** -0.5 if j < NC else 1.0)
                    if s == 8 and has("prev", it):
                        for c in range(NC):
                            take(f"x2t{c}", it, x2T[:, c, :])
                    if s in (9, 10, 11, 12) and has("prev", it):
                        m = 2 * (s - 9)
                        take(f"ffn{m}", it, act_T[:, m, :], func=ACT.Relu)

            act.activation(bqk_sb[:, 0:NC], bqk_sb[:, 0:NC], ACT.Copy, scale=HD ** -0.5).then_inc(bias_scaled, 1)
            act.wait_ge(bias_scaled, 1)
            iterations(act, body)

        @block.vector
        def _(dve):
            steps = [0]

            def step(ins):
                steps[0] += 1
                ins.then_inc(dve_step, 1)
                dve.wait_ge(dve_step, steps[0])

            dve.wait_ge(pool_step, 2)
            step(dve.tensor_copy(dist_f, dist_i))
            step(dve.tensor_scalar(dist_i.bitcast(F32), dist_f, -1.0, None, ALU.mult))
            step(dve.tensor_tensor(dist_f, dist_f, dist_i.bitcast(F32), ALU.max))
            for h in range(H):
                slope = float(np.power(np.float32(2.0), np.float32(-8.0 * h / H)))
                step(dve.tensor_scalar(dist[:, h, :], dist_f, -slope, None, ALU.mult))

            dve.wait_ge(weights_loaded, 16 * 11)
            for w, n, width, scale, half in ((w1_nat, NM, D, scale1, half1), (w2_nat, NC, HID, scale2, half2)):
                step(dve.tensor_reduce(scale[:, :], w, AX.X, ALU.add, apply_absolute_value=True))
                step(dve.tensor_scalar(scale[:, :], scale[:, :], 1.0 / width, 1e-5, ALU.mult, ALU.max))
                step(dve.tensor_scalar(half[:, 0, :], scale[:, :], 0.5, None, ALU.mult))
                step(dve.tensor_scalar(half[:, 1, :], scale[:, :], -0.5, None, ALU.mult))
                pos = t_pos.rearrange("p (n w) -> p n w", n=n)
                neg = t_neg.rearrange("p (n w) -> p n w", n=n)
                for i in range(n):
                    step(dve.tensor_scalar(pos[:, i, :], w[:, i, :], half[:, 0, i:i + 1], None, ALU.is_gt))
                    step(dve.tensor_scalar(neg[:, i, :], w[:, i, :], half[:, 1, i:i + 1], None, ALU.is_lt))
                step(dve.tensor_tensor(pos, pos, neg, ALU.subtract))
                step(dve.tensor_tensor(pos, pos, w, ALU.subtract))
                step(dve.tensor_tensor(w, w, pos, ALU.add))
            for c in range(NC):
                step(dve.tensor_scalar(w2_nat[:, c, :], w2_nat[:, c, :], scale2[:, c:c + 1], None, ALU.mult))
            dve.wait_ge(rows_ready, 2)
            dve.wait_ge(filled[0], 1)
            dve.tensor_scalar(low_bv, bank[0][0:RANK, 0:D], gate_bc[0:RANK, :], None,
                              ALU.mult).then_inc(drained[0], 1)
            for m in range(NM):
                k = m % 2
                dve.wait_ge(low_filled, m + 1)
                dve.scalar_tensor_tensor(out=w1_nat[:, m, :], in0=w1_nat[:, m, :], scalar=scale1[:, m:m + 1],
                                         in1=turn_ps[k][:, 0:D], op0=ALU.mult, op1=ALU.add).then_inc(low_ready, 1)
            for n in range(8):
                k, use = SETUP_BANKS[n]
                dve.wait_ge(filled[k], use + 1)
                if n < 4:
                    c, m = n // 2, 4 * (n % 2)
                    dst = w1T[:, c, m * P:(m + 4) * P]
                else:
                    m = 2 * (n - 4)
                    dst = w2T[:, m:m + 2, :].rearrange("p m d -> p (m d)")
                dve.tensor_copy(dst, bank[k][:, :]).then_inc(drained[k], 1)

            def take(name, it, fn):
                take_wait(dve, name, it)
                k = BANK_OF[name]
                fn(bank[k]).then_inc(drained[k], 1)

            def bias_and_max(b, h):
                for t in range(NT):
                    wait_alone(dve, scores_ready, b * (NT * H) + NT * h + t + 1)
                    if t == 0 and not (isinstance(b, int) and b == 0 and h < 2):
                        wait_alone(dve, probs_ready, b * (NT * H) + NT * (h - 1))
                    dve.tensor_tensor_reduce(nscore[0:rows(t), h % 2, t, :],
                                             score_ps[(NT * h + t) % 2][0:rows(t), 0:S],
                                             dist[0:rows(t), h, (2 - t) * P:(2 - t) * P + S],
                                             -1.0, 3.0e38, ALU.add, ALU.min,
                                             nmax[0:rows(t), h % 2, t:t + 1]).then_inc(scores_taken, 1)

            def layer_norm(k, src, n):
                for t in range(NT):
                    last = dve.bn_stats(stats[:, k, t, :], src[:, t, :])
                last.then_inc(stats_done[k], 1)
                wait_alone(dve, stats_done[k], n + 1)
                for t in range(NT):
                    last = dve.bn_aggr(moments[:, k, t, :], stats[:, k, t, :])
                last.then_inc(moments_done[k], 1)

            def normalize(k, dst, src, n, ready):
                dve.wait_ge(rstd_ready[k], n + 1)
                dve.wait_ge(moments_done[k], n + 1)
                for t in range(NT):
                    last = dve.tensor_scalar(dst[:, t, :], src[:, t, :], moments[:, k, t, 0:1],
                                             rstd[:, k, t:t + 1], ALU.subtract, ALU.mult)
                last.then_inc(ready, 1)

            def head_outputs(b, g, it):
                name = f"otok{g}"
                take_wait(dve, name, it)
                k = BANK_OF[name]
                ps = bank[k][:, 0:SP3].rearrange("p (t j c) -> p t j c", t=NT, j=4)
                dve.reciprocal(recip[:, :, :], ps[:, :, :, HD]).then_inc(recip_ready, 1)
                dve.wait_ge(recip_ready, b * 4 + g + 1)
                dve.tensor_tensor(o_norm[:, :, 64 * g:64 * g + 64].rearrange("p t (j c) -> p t j c", j=4),
                                  ps[:, :, :, 0:HD],
                                  recip[:, :, :].rearrange("p t (j c) -> p t j c", c=1).to_broadcast([P, NT, 4, HD]),
                                  ALU.mult).then_inc(drained[k], 1)

            def body(it):
                nxt, prv = it + 1, it - 1
                for s in range(H):
                    if has("own", it):
                        bias_and_max(it, s)
                    if (two := lagged(it, s, 2)) and (has("own", it) or (s < 2 and it == B)):
                        b, h = two
                        if not (isinstance(b, int) and b == 0 and h < RING):
                            dve.wait_ge(o_ready, b * 4 + h // 4 - 1)
                        k, n = turn(b, h, 1)
                        dve.wait_ge(turned[k], n)
                        dve.tensor_copy(probsT[0:rows(1), h % RING, 1, :],
                                        turn_ps[k][0:rows(1), 0:S]).then_inc(turned_taken[k], 1)
                    if s == 0 and has("prev", it):
                        head_outputs(prv, 2, it)
                    if s == 3 and has("next", it):
                        dve.wait_ge(tokens_ready, nxt + 1)
                        layer_norm(0, h_new, nxt)
                    if s == 4:
                        if has("prev", it):
                            head_outputs(prv, 3, it)
                        if has("own", it):
                            for t in range(NT):
                                take(f"v{t}", it, lambda ps: dve.tensor_tensor(
                                    v_sb[:, t, :, 0:HD], ps[:, 0:D].rearrange("p (h c) -> p h c", h=H),
                                    bias_bc[:, 0, :].rearrange("p (h c) -> p h c", h=H), ALU.add))
                        if has("next", it):
                            normalize(0, xn, h_new, nxt, xn_ready)
                    if s == 5 and has("prev", it):
                        for c in range(NC):
                            take(f"ont{c}", it, lambda ps: dve.tensor_copy(o_normT[:, c, :], ps[:, 0:SP3]))
                    if s == 6 and has("prev", it):
                        dve.wait_ge(h_old_loaded, it * 16)
                        take("proj0", it, lambda ps: dve.tensor_tensor(
                            h_mid[:, 0:2, :].rearrange("p t d -> p (t d)"), ps[:, :],
                            h_old[:, 0:2, :].rearrange("p t d -> p (t d)"), ALU.add))
                        take("proj1", it, lambda ps: dve.tensor_tensor(h_mid[:, 2, :], ps[:, 0:D],
                                                                       h_old[:, 2, :], ALU.add))
                        step_taken(dve, "proj1", it)
                        layer_norm(1, h_mid, prv)
                    if s == 7 and has("prev", it):
                        dve.wait_ge(stored, it * 32)
                        normalize(1, x2, h_mid, prv, x2_ready)
                    if s == 8:
                        if has("own", it):
                            head_outputs(it, 0, it)
                        if has("next", it):
                            for j in range(NQ):
                                step_taken(dve, f"qk{j}", it)
                            dve.tensor_copy(qk_parts[:, 0, :, :], qk[:, :, :]).then_inc(high_ready, 1)
                    if s in (9, 10, 11, 12):
                        if s == 12 and has("own", it):
                            head_outputs(it, 1, it)
                        if has("prev", it):
                            m = 2 * (s - 9) + 1
                            take(f"ffn{m}", it, lambda ps: dve.tensor_scalar(act_T[:, m, :], ps[:, 0:S], 0.0, None,
                                                                             ALU.max))
                    if s == 10 and has("next", it):
                        dve.wait_ge(rest_ready, nxt + 1)
                        dve.tensor_copy(qk_parts[:, 1, :, :], rest[:, :, :]).then_inc(middle_ready, 1)
                    if s in (13, 14, 15) and has("prev", it):
                        t = s - 13
                        take(f"y{t}", it, lambda ps: dve.tensor_tensor(
                            y_sb[0:rows(t), t, :], ps[0:rows(t), 0:D], h_mid[0:rows(t), t, :], ALU.add))

            iterations(dve, body)

        @block.tensor
        def _(pe):
            pe.wait_ge(consts_ready, 2)
            pe.wait_ge(weights_loaded, 16 * 11)
            pe.matmul(bank[0][0:RANK, 0:D], low_bT, low_v, start=True, stop=True).then_inc(filled[0], 1)
            pe.wait_ge(drained[0], 1)
            for m in range(NM):
                k = m % 2
                if m >= 2:
                    pe.wait_ge(low_ready, m - 1)
                pe.matmul(turn_ps[k][:, 0:D], low_uT[:, m * P:(m + 1) * P], low_bv, start=True,
                          stop=True).then_inc(low_filled, 1)
            pe.wait_ge(low_ready, NM)
            for n in range(8):
                k, use = SETUP_BANKS[n]
                if use:
                    pe.wait_ge(drained[k], use)
                for i in range(4):
                    if n < 4:
                        src = w1_nat[:, 4 * (n % 2) + i, (n // 2) * P:(n // 2 + 1) * P]
                    else:
                        m, c = 2 * (n - 4) + i // 2, i % 2
                        src = w2_nat[:, c, m * P:(m + 1) * P]
                    last = pe.transpose(bank[k][:, i * P:(i + 1) * P], src, ident[:, :])
                last.then_inc(filled[k], 1)

            def scores(b, h):
                for half in range(2):
                    if h == HALF * half:
                        pe.wait_ge(aug_loaded[half], b * 192 + 192)
                for t in range(NT):
                    n = NT * h + t
                    if not (isinstance(b, int) and b == 0 and n < 2):
                        pe.wait_ge(scores_taken, b * (NT * H) + n - 1)
                    pe.matmul(score_ps[n % 2][0:rows(t), 0:S], q_aug[:, h, t * P:t * P + rows(t)], k_aug[:, h, :],
                              start=True, stop=True).then_inc(scores_ready, 1)

            def transpose_probs(b, h):
                pe.wait_ge(probs_ready, b * (NT * H) + NT * (h + 1))
                for u in range(NT):
                    k, n = turn(b, h, u)
                    if not (isinstance(b, int) and b == 0 and NT * h + u < 2):
                        pe.wait_ge(turned_taken[k], n - 1)
                    for t in range(NT):
                        last = pe.transpose(turn_ps[k][0:rows(u), t * P:t * P + rows(t)],
                                            probs[0:rows(t), h % 2, t, u * P:u * P + rows(u)],
                                            ident[0:rows(t), 0:rows(t)])
                    last.then_inc(turned[k], 1)

            def times_v(b, g):
                for k in range(2):
                    pe.wait_ge(turned_taken[k], b * (NT * H // 2) + 6 * (g + 1))
                if not (isinstance(b, int) and b == 0 and g == 0):
                    pe.wait_ge(o_taken, b * 4 + g)
                if g == 0:
                    for t in range(NT):
                        step_taken(pe, f"v{t}", b)
                for u in range(NT):
                    for j in range(4):
                        h = 4 * g + j
                        last = pe.matmul(o_ps[32 * j:32 * j + 32, 0:S], v_sb[0:rows(u), u, h, :],
                                         probsT[0:rows(u), h % RING, u, :], start=(u == 0), stop=(u == NT - 1))
                last.then_inc(o_ready, 1)

            def fill(name, it, fn):
                fill_wait(pe, name, it)
                k = BANK_OF[name]
                fn(bank[k]).then_inc(filled[k], 1)

            def transpose_rows(src, c):
                def fn(ps):
                    for t in range(NT):
                        last = pe.transpose(ps[:, t * P:(t + 1) * P], src[:, t, c * P:(c + 1) * P], ident[:, :])
                    return last
                return fn

            def sum_over_chunks(dst, lhs, rhs, n=NC):
                for c in range(n):
                    last = pe.matmul(dst, lhs(c), rhs(c), start=(c == 0), stop=(c == n - 1))
                return last

            def head_outputs(b, g, it):
                pe.wait_ge(o_taken, b * 4 + g + 1)

                def fn(ps):
                    for t in range(NT):
                        last = pe.transpose(ps[:, t * P:(t + 1) * P], oT[:, t * P:(t + 1) * P], ident[:, :])
                    return last
                fill(f"otok{g}", it, fn)

            def body(it):
                nxt, prv = it + 1, it - 1
                for s in range(H):
                    if has("own", it):
                        scores(it, s)
                    if (two := lagged(it, s, 2)) and (has("own", it) or (s < 2 and it == B)):
                        transpose_probs(*two)
                    if s % 4 == 3 and (got := lagged(it, s, 7)) and (has("own", it) or (s == 3 and it == B)):
                        times_v(got[0], got[1] // 4)
                    if s == 0 and has("prev", it):
                        head_outputs(prv, 2, it)
                    if s == 4:
                        if has("prev", it):
                            head_outputs(prv, 3, it)
                        if has("own", it):
                            for t in range(NT):
                                fill(f"v{t}", it, lambda ps: sum_over_chunks(
                                    ps[:, 0:D], lambda c: xT[:, c, t * P:(t + 1) * P],
                                    lambda c: wqkv_sb[:, c, 2 * D:3 * D]))
                    if s == 5:
                        if has("next", it):
                            pe.wait_ge(xn_ready, nxt + 1)
                            for c in range(NC):
                                fill(f"xt{c}", it, transpose_rows(xn, c))
                        if has("prev", it):
                            step_taken(pe, "otok3", it)
                            for c in range(NC):
                                fill(f"ont{c}", it, transpose_rows(o_norm, c))
                    if s in (6, 7) and has("next", it):
                        for j in (0, 1) if s == 6 else (2, 3):
                            if j == 0:
                                for c in range(NC):
                                    step_taken(pe, f"xt{c}", it)
                            fill(f"qk{j}", it, lambda ps: sum_over_chunks(
                                ps[:, 0:S], lambda c: wqkv_sb[:, c, j * P:(j + 1) * P], lambda c: xT[:, c, 0:S]))
                    if s == 6 and has("prev", it):
                        for c in range(NC):
                            step_taken(pe, f"ont{c}", it)

                        def proj(ps, tiles):
                            for i, t in enumerate(tiles):
                                last = sum_over_chunks(ps[:, i * D:(i + 1) * D],
                                                       lambda c: o_normT[:, c, t * P:(t + 1) * P],
                                                       lambda c: wo_sb[:, c, :])
                            return last
                        fill("proj0", it, lambda ps: proj(ps, (0, 1)))
                        fill("proj1", it, lambda ps: proj(ps, (2,)))
                    if s == 8:
                        if has("own", it):
                            head_outputs(it, 0, it)
                        if has("prev", it):
                            pe.wait_ge(x2_ready, it)
                            for c in range(NC):
                                fill(f"x2t{c}", it, transpose_rows(x2, c))
                    if s in (9, 10, 11, 12):
                        if s == 12 and has("own", it):
                            head_outputs(it, 1, it)
                        if has("prev", it):
                            if s == 9:
                                for c in range(NC):
                                    step_taken(pe, f"x2t{c}", it)
                            for m in (2 * (s - 9), 2 * (s - 9) + 1):
                                fill(f"ffn{m}", it, lambda ps: sum_over_chunks(
                                    ps[:, 0:S], lambda c: w1T[:, c, m * P:(m + 1) * P], lambda c: x2T[:, c, 0:S]))
                    if s in (13, 14, 15) and has("prev", it):
                        t = s - 13
                        pe.wait_ge(squares_ready, it * (NM // 2))
                        fill(f"y{t}", it, lambda ps: sum_over_chunks(
                            ps[0:rows(t), 0:D], lambda m: act_T[:, m, t * P:t * P + rows(t)],
                            lambda m: w2T[:, m, :], n=NM))

            iterations(pe, body)


def kernel(**inputs):
    import concourse.bacc as bacc
    from concourse.bass_utils import run_bass_kernel_spmd

    a = {n: np.asarray(v) for n, v in inputs.items()}
    order = np.arange(2 * D).reshape(NQ, HALF, HD).transpose(0, 2, 1).reshape(-1)
    order = np.concatenate([order, np.arange(2 * D, 3 * D)])
    arrays = {
        "x_dram": a["x"],
        "txt_dram": a["txt"],
        "wqkvT_dram": np.ascontiguousarray(a["L0_attn_W_qkv"][order].T),
        "bqk_dram": np.ascontiguousarray(a["L0_attn_b_qkv"][order[:2 * D]].reshape(NQ, P).T),
        "bv_dram": np.ascontiguousarray(a["L0_attn_b_qkv"][2 * D:].reshape(1, D)),
        "woT_dram": np.ascontiguousarray(a["L0_attn_W_out"].T),
        "bo_dram": np.ascontiguousarray(a["L0_attn_b_out"].reshape(1, D)),
        "fast_bT_dram": np.ascontiguousarray(a["L0_ffn_fast_b"].T),
        "w_fc_dram": a["L0_ffn_w_fc"],
        "w_proj_dram": a["L0_ffn_w_proj"],
        "uT_dram": np.ascontiguousarray(a["L0_ffn_u"].T),
        "v_dram": a["L0_ffn_v"],
        "gate_dram": np.ascontiguousarray(a["L0_ffn_gate"].reshape(1, 1)),
    }
    nc = bacc.Bacc("TRN2", target_bir_lowering=False, num_devices=1)
    args = [nc.dram_tensor(n, v.shape, mybir.dt.from_np(v.dtype), kind="ExternalInput").ap()
            for n, v in arrays.items()]
    out = nc.dram_tensor("out_dram", (B, S, D), F32, kind="ExternalOutput").ap()
    early_fusion_kernel(nc, *args, out)
    return run_bass_kernel_spmd(nc, [arrays], core_ids=[0]).results[0]["out_dram"]
```

```python
from contextlib import ExitStack

import numpy as np

import concourse.bass as bass
from concourse import mybir

F32 = mybir.dt.float32
BF16 = mybir.dt.bfloat16
F32R = mybir.dt.float32r
I32 = mybir.dt.int32
ALU = mybir.AluOpType
ACT = mybir.ActivationFunctionType
AX = mybir.AxisListType

B, IMG, TXT, D = 32, 256, 77, 256
S = IMG + TXT
P = 128
ROWS = [P, P, S - 2 * P]
NT = len(ROWS)
SP3 = NT * P
H, HD = 16, 16
HID, RANK = 1024, 16
NC = D // P
NM = HID // P
HALF = H // 2
EPS = 1e-5
Q_PARTS = [0, 0, 1, 1, 0, 2]
K_PARTS = [0, 1, 0, 1, 2, 0]
KAUG = HD * len(Q_PARTS)
RING = 8
NQ = 2 * NC
SE = S + 1
BW = S + 2 * P
QK_SLOTS = {6: (0,), 8: (1, 2), 10: (3,)}
FFN_SLOTS = {10: (0, 1), 12: (2, 3), 13: (4, 5), 14: (6, 7)}
SQUARE_SLOTS = {11: 0, 13: 2, 14: 4, 15: 6}
ONT_SLOTS = {1: 0, 5: 1}
Y_SLOTS = {0: 0, 1: 1, 2: 2}

USES = [
    ("otok2", "prev"), ("y0", "late"), ("ont0", "prev"), ("y1", "late"), ("y2", "late"), ("pv3", "prev"),
    ("otok3", "prev"), ("v01", "own"), ("v2", "own"), ("ont1", "prev"), ("xt0", "next"), ("xt1", "next"),
    ("qk0", "next"), ("proj0", "prev"), ("proj1", "prev"), ("pv0", "own"),
    ("qk1", "next"), ("qk2", "next"), ("x2t0", "prev"), ("x2t1", "prev"), ("otok0", "own"), ("qk3", "next"),
    ("ffn0", "prev"), ("ffn1", "prev"), ("pv1", "own"), ("otok1", "own"),
    ("ffn2", "prev"), ("ffn3", "prev"), ("ffn4", "prev"), ("ffn5", "prev"), ("ffn6", "prev"), ("ffn7", "prev"),
    ("pv2", "own"),
]
BANKS = 3
BANK_OF = {name: i % BANKS for i, (name, _) in enumerate(USES)}
assert len(USES) % BANKS == 0
SETUP_BANKS = [((n + 1) % BANKS, (n + 1) // BANKS) for n in range(9)]
LOOP_FIRST, LOOP_END = 2, B - 2


def parts_of(it):
    if not isinstance(it, int):
        return ("own", "prev", "late", "next", "load")
    here = (("own", 0 <= it < B), ("prev", 1 <= it <= B), ("late", 2 <= it <= B + 1), ("next", it < B - 1),
            ("load", it < B - 2))
    return tuple(p for p, on in here if on)


def uses_in(k, it, before=None):
    n = 0
    for name, part in USES:
        if name == before:
            break
        n += BANK_OF[name] == k and part in parts_of(it)
    return n


def bank_uses_before(name, it, back=0):
    if back and isinstance(it, int):
        return bank_uses_before(name, it - 1)
    k = BANK_OF[name]
    whole = it if isinstance(it, int) else LOOP_FIRST
    n = (10 + BANKS - 1 - k) // BANKS + sum(uses_in(k, i) for i in range(-1, whole)) + uses_in(k, it, before=name)
    if isinstance(it, int):
        return n
    return (it - LOOP_FIRST) * uses_in(k, it) + n - back * uses_in(k, it)


def early_fusion_kernel(nc, x, txt, wqkvT, bqk, q_scale, bv, woT, bo, fast_bT, w_fc, w_proj, uT, v, gate, out):
    ctx = ExitStack()
    with ctx:
        def sb(name, shape, dt=F32):
            return ctx.enter_context(nc.sbuf_tensor(name, shape, dt))

        def psum(name):
            return ctx.enter_context(nc.psum_tensor(name, [P, 512], F32))

        def sem(name):
            return ctx.enter_context(nc.semaphore(name))

        def pair(name, shape):
            return [sb(f"{name}_{part}", shape, F32R) for part in ("high", "low")]

        wqkv = pair("wqkv", [P, NC, 3 * D])
        wo = pair("wo", [P, NC, D])
        w1T = pair("w1T", [P, NC, HID])
        w2T = sb("w2T", [P, NM, D], F32R)
        scale2_bc = sb("scale2_bc", [P, D])
        qscale_sb = sb("qscale_sb", [P, NC])
        bqk_sb = sb("bqk_sb", [P, NQ])
        bias_bc = sb("bias_bc", [P, 2, D])
        ident = sb("ident", [P, P])
        dist = sb("dist", [P, BW])
        mhalf = sb("mhalf", [P, NT])

        imgA = sb("imgA", [P, 2, IMG + 1])
        imgB = sb("imgB", [P, 2, IMG + 1])
        edges = sb("edges", [P, 2, 2, IMG])
        h_new = sb("h_new", [P, NT, D])
        h_bias = sb("h_bias", [P, NT, D])
        h_old = sb("h_old", [P, NT, D])
        stats = sb("stats", [P, 2, NT, 6])
        moments = sb("moments", [P, 2, NT, 2])
        var_eps = sb("var_eps", [P, 2, NT])
        rstd = sb("rstd", [P, 2, NT])
        xn = sb("xn", [P, NT, D])
        xT = pair("xT", [P, NC, SP3])
        qk = sb("qk", [P, NQ, S])
        qk_parts = sb("qk_parts", [P, 3, NQ, S], BF16)
        q_aug = sb("q_aug", [KAUG, H, S], BF16)
        k_aug = sb("k_aug", [KAUG, H, S], BF16)

        v_sb = sb("v_sb", [P, NT, H, 32])
        nscore = sb("nscore", [P, 2, NT, S])
        nmax = sb("nmax", [P, 2, NT])
        probs = sb("probs", [P, 2, NT, S])
        probsT = sb("probsT", [P, RING, NT, S])
        oT = sb("oT", [P, SP3])
        recip = sb("recip", [P, NT, 4])
        o_norm = sb("o_norm", [P, NT, D])

        o_normT = pair("o_normT", [P, NC, SP3])
        h_mid = sb("h_mid", [P, NT, D])
        x2 = sb("x2", [P, NT, D])
        x2T = pair("x2T", [P, NC, SP3])
        relu_T = sb("relu_T", [P, 4, S])
        act_T = pair("act_T", [P, NM, S])
        y_sb = x2

        flat = probsT[:, :, :, :].rearrange("p r t s -> p (r t s)")
        w1_nat = flat[:, 0:NM * D].rearrange("p (m d) -> p m d", m=NM)
        w2_nat = flat[:, NM * D:2 * NM * D].rearrange("p (c m) -> p c m", c=NC)
        t_pos = flat[:, 2 * NM * D:3 * NM * D]
        wqkv_raw = flat[:, 3 * NM * D:3 * NM * D + NC * 3 * D].rearrange("p (c n) -> p c n", c=NC)
        wo_raw = nscore[:, :, :, :].rearrange("p r t s -> p (r t s)")[:, 2 * BW:2 * BW + NC * D] \
            .rearrange("p (c n) -> p c n", c=NC)
        t_neg = qk[:, :, :].rearrange("p j s -> p (j s)")[:, 0:HID]
        scale2_cols = [relu_T[:, c, 0:P] for c in range(NC)]
        dist_i = nscore[:, :, :, :].rearrange("p r t s -> p (r t s)")[:, 0:BW].bitcast(I32)
        dist_f = nscore[:, :, :, :].rearrange("p r t s -> p (r t s)")[:, BW:2 * BW]
        low_uT = probs[0:RANK, :, :, :].rearrange("p r t s -> p (r t s)")[:, 0:HID]
        low_v = xn[0:RANK, 0, :]
        low_bT = xn[0:RANK, 1, 0:RANK]
        low_bv = xn[0:RANK, 2, :]
        gate_bc = recip[:, 0, 0:1]
        bias_row = y_sb[0:1, :, :].rearrange("p t d -> p (t d)")[:, 0:2 * D + 1]
        scale1 = sb("scale1", [P, NM])
        half1 = sb("half1", [P, 2, NM])
        scale2 = sb("scale2", [P, NC])
        half2 = sb("half2", [P, 2, NC])

        score_ps = [psum(f"score_ps{t}") for t in range(NT)]
        turn_ps = [psum("turn_ps0"), psum("turn_ps1")]
        bank = [psum(f"bank{k}") for k in range(BANKS)]

        waits_met = sem("waits_met")
        weights_loaded = sem("weights_loaded")
        pool_step = sem("pool_step")
        consts_ready = sem("consts_ready")
        rows_ready = sem("rows_ready")
        dve_step = sem("dve_step")
        low_filled = sem("low_filled")
        low_ready = sem("low_ready")
        bias_scaled = sem("bias_scaled")
        scale2_ready = sem("scale2_ready")
        filled = [sem(f"bank_filled{k}") for k in range(BANKS)]
        drained = [sem(f"bank_drained{k}") for k in range(BANKS)]
        tokens_loaded = sem("tokens_loaded")
        edges_ready = sem("edges_ready")
        edges_abs = sem("edges_abs")
        edges_sum = sem("edges_sum")
        tokens_ready = sem("tokens_ready")
        stats_done = [sem("stats1_done"), sem("stats2_done")]
        moments_done = [sem("moments1_done"), sem("moments2_done")]
        eps_added = [sem("eps1_added"), sem("eps2_added")]
        rstd_ready = [sem("rstd1_ready"), sem("rstd2_ready")]
        xn_ready = sem("xn_ready")
        x2_ready = sem("x2_ready")
        h_bias_ready = sem("h_bias_ready")
        h_old_loaded = sem("h_old_loaded")
        xT_high = sem("xT_high")
        high_ready = sem("high_ready")
        rest_ready = sem("rest_ready")
        middle_ready = sem("middle_ready")
        low_part_ready = sem("low_part_ready")
        aug_loaded = [sem("aug_loaded0"), sem("aug_loaded1")]
        scores_ready = sem("scores_ready")
        scores_taken = sem("scores_taken")
        probs_ready = sem("probs_ready")
        turned = [sem("turned0"), sem("turned1")]
        turned_taken = [sem("turned_taken0"), sem("turned_taken1")]
        recip_ready = sem("recip_ready")
        o_normT_high = sem("o_normT_high")
        x2T_high = sem("x2T_high")
        squared = sem("squared")
        square_high = sem("square_high")
        y_summed = sem("y_summed")
        squares_ready = sem("squares_ready")
        stored = sem("stored")

        def fill_wait(eng, name, it):
            n = bank_uses_before(name, it)
            if not (isinstance(n, int) and n == 0):
                eng.wait_ge(drained[BANK_OF[name]], n)

        def take_wait(eng, name, it, back=0):
            eng.wait_ge(filled[BANK_OF[name]], bank_uses_before(name, it, back) + 1)

        def wait_alone(eng, semaphore, value):
            eng.wait_ge(semaphore, value)
            if not isinstance(value, int):
                eng.sem_inc(waits_met, 1)

        def step_taken(eng, name, it, back=0):
            wait_alone(eng, drained[BANK_OF[name]], bank_uses_before(name, it, back) + 1)

        def ring_wait(eng, it, s):
            group = (s - 2) // 4 - RING // 4
            back = int(group < -1)
            if not (isinstance(it, int) and it - back < (1 if group % 4 == 3 else 0)):
                take_wait(eng, f"pv{group % 4}", it, back)

        def rows(t):
            return ROWS[t]

        def slope(h):
            return float(np.power(np.float32(2.0), np.float32(-8.0 * h / H)))

        def lagged(b, s, lag):
            if s >= lag:
                return b, s - lag
            if isinstance(b, int) and b == 0:
                return None
            return b - 1, s - lag + H

        def turn(b, h, u):
            m = NT * h + u
            return m % 2, b * (NT * H // 2) + m // 2 + 1

        def iterations(eng, body):
            for it in range(-1, LOOP_FIRST):
                body(it)
            with eng.Fori(LOOP_FIRST, LOOP_END) as it:
                body(it)
            for it in range(LOOP_END, B + 2):
                body(it)

        def has(part, it):
            return part in parts_of(it)

        block = ctx.enter_context(nc.Block())

        @block.sync
        def _(sp):
            loads = [
                (wqkv_raw, wqkvT.rearrange("(c p) n -> p c n", p=P)),
                (wo_raw, woT.rearrange("(c p) n -> p c n", p=P)),
                (bqk_sb[:, :], bqk), (qscale_sb[:, :], q_scale),
                (w1_nat, w_fc.rearrange("(m p) d -> p m d", p=P)),
                (w2_nat, w_proj.rearrange("(c p) m -> p c m", p=P)),
                (low_uT, uT), (low_v, v), (low_bT, fast_bT),
                (bias_row[:, 0:D], bv), (bias_row[:, D:2 * D], bo), (bias_row[:, 2 * D:2 * D + 1], gate),
            ]
            sp.sem_inc(stored, 32)
            for dst, src in loads:
                sp.dma_start(dst, src).then_inc(weights_loaded, 16)
            sp.wait_ge(consts_ready, 1)

            def load_tokens(n):
                img = x[n, 0]
                sp.dma_start(imgA[:, :, 0:IMG], img.rearrange("(t p) c -> p t c", p=P)).then_inc(tokens_loaded, 16)
                sp.dma_start(imgB[:, 0, 0:IMG], img[1:P + 1, :]).then_inc(tokens_loaded, 16)
                sp.dma_start(imgB[0:112, 1, 0:IMG], img[P + 1:P + 113, :]).then_inc(tokens_loaded, 16)
                sp.dma_start(imgB[112:127, 1, 0:IMG], img[P + 113:IMG, :]).then_inc(tokens_loaded, 16)
                sp.dma_start(h_new[0:TXT, 2, :], txt[n]).then_inc(tokens_loaded, 16)

            def load_aug(half, parts=range(3)):
                for part in parts:
                    for aug, used, block_ in ((q_aug, Q_PARTS, half), (k_aug, K_PARTS, 2 + half)):
                        for i in (i for i, p in enumerate(used) if p == part):
                            sp.dma_start(aug[HD * i:HD * (i + 1), HALF * half:HALF * (half + 1), :],
                                         qk_parts[:, part, block_, :]).then_inc(aug_loaded[half], 16)

            def body(it):
                if isinstance(it, int) and it == -1:
                    load_tokens(0)
                if has("late", it):
                    wait_alone(sp, y_summed, it - 1)
                    sp.dma_start(out[it - 2, 0:2 * P, :].rearrange("(t p) d -> p t d", p=P),
                                 y_sb[:, 0:2, :]).then_inc(stored, 16)
                    sp.dma_start(out[it - 2, 2 * P:S, :], y_sb[0:TXT, 2, :]).then_inc(stored, 16)
                if has("own", it):
                    wait_alone(sp, h_bias_ready, it + 1)
                    if has("prev", it):
                        step_taken(sp, "proj1", it)
                    sp.dma_start(h_old[:, :, :], h_bias[:, :, :]).then_inc(h_old_loaded, 16)
                if has("load", it):
                    wait_alone(sp, xn_ready, it + 2)
                    wait_alone(sp, h_bias_ready, it + 2)
                    load_tokens(it + 2)
                if has("next", it):
                    if has("own", it):
                        wait_alone(sp, scores_ready, it * (NT * H) + NT * HALF)
                    for part, ready in enumerate((high_ready, middle_ready, low_part_ready)):
                        wait_alone(sp, ready, it + 2)
                        load_aug(0, (part,))
                    if has("own", it):
                        wait_alone(sp, scores_ready, it * (NT * H) + NT * H)
                    load_aug(1)

            iterations(sp, body)
            sp.wait_ge(stored, 32 * (B + 1))

        @block.gpsimd
        def _(pool):
            pool.memset(imgA[:, :, :], 0.0)
            pool.memset(imgB[:, :, :], 0.0)
            pool.memset(h_new[:, :, :], 0.0)
            pool.memset(oT[:, :], 1.0)
            pool.memset(v_sb[:, :, :, HD:HD + 1], 1.0)
            pool.memset(v_sb[:, :, :, HD + 1:32], 0.0)
            pool.memset(mhalf[:, :], -0.5).then_inc(consts_ready, 1)
            pool.memset(ident[:, :], 0.0).then_inc(pool_step, 1)
            pool.iota(dist_i, pattern=[[1, BW]], base=-2 * P, channel_multiplier=-1).then_inc(pool_step, 1)
            pool.wait_ge(pool_step, 2)
            pool.affine_select(out=ident[:, :], in_=ident[:, :], compare_op=ALU.not_equal, fill=1.0,
                               base=0, pattern=[[-1, P]], channel_multiplier=1).then_inc(consts_ready, 1)
            pool.wait_ge(weights_loaded, 16 * 12)
            pool.partition_broadcast(bias_bc[:, :, :].rearrange("p a d -> p (a d)"), bias_row[:, 0:2 * D],
                                     channels=P).then_inc(rows_ready, 1)
            pool.partition_broadcast(gate_bc, bias_row[:, 2 * D:2 * D + 1], channels=P).then_inc(rows_ready, 1)
            pool.wait_ge(rows_ready, 2)

            def make_rstd(k, n):
                wait_alone(pool, moments_done[k], n + 1)
                pool.tensor_scalar(var_eps[:, k, :], moments[:, k, :, 1], EPS, None, ALU.add).then_inc(eps_added[k], 1)
                pool.wait_ge(eps_added[k], n + 1)
                pool.tensor_tensor(rstd[:, k, :], var_eps[:, k, :], mhalf[:, :], ALU.pow).then_inc(rstd_ready[k], 1)

            def low_squares(it, chunks):
                for m in chunks:
                    pool.wait_ge(square_high, (it - 1) * 4 + m // 2 + 1)
                    pool.tensor_tensor(act_T[1][:, m:m + 2, :], relu_T[:, m % 4:m % 4 + 2, :],
                                       act_T[0][:, m:m + 2, :].bitcast(F32), ALU.subtract).then_inc(squares_ready, 1)

            def differences(n):
                pool.wait_ge(tokens_loaded, n * 80 + 80)
                pool.tensor_tensor(edges[:, 0, :, :], imgA[:, :, 0:IMG], imgB[:, :, 1:IMG + 1], ALU.subtract)
                pool.tensor_tensor(edges[:, 1, :, :], imgB[:, :, 0:IMG], imgA[:, :, 1:IMG + 1],
                                   ALU.subtract).then_inc(edges_ready, 1)

            def body(it):
                nxt = it + 1
                if isinstance(it, int) and it == -1:
                    differences(0)
                if has("next", it):
                    pool.wait_ge(edges_abs, nxt + 1)
                    pool.tensor_tensor(edges[:, 0, :, :], edges[:, 0, :, :], edges[:, 1, :, :],
                                       ALU.add).then_inc(edges_sum, 1)
                    wait_alone(pool, edges_sum, nxt + 1)
                    pool.tensor_scalar(h_new[:, 0:2, :], edges[:, 0, :, :], 0.0, 1.0, ALU.max,
                                       ALU.min).then_inc(tokens_ready, 1)
                if has("next", it):
                    make_rstd(0, nxt)
                if has("late", it):
                    for t in range(NT):
                        step_taken(pool, f"y{t}", it)
                    pool.tensor_tensor(y_sb[:, :, :], y_sb[:, :, :], h_mid[:, :, :], ALU.add).then_inc(y_summed, 1)
                if has("prev", it):
                    make_rstd(1, it - 1)
                if has("next", it):
                    if has("own", it):
                        pool.wait_ge(h_old_loaded, it * 16 + 16)
                    pool.tensor_tensor(h_bias[:, :, :], h_new[:, :, :],
                                       bias_bc[:, 1:2, :].to_broadcast([P, NT, D]),
                                       ALU.add).then_inc(h_bias_ready, 1)
                if has("load", it):
                    differences(it + 2)
                if has("next", it):
                    pool.wait_ge(high_ready, nxt + 1)
                    pool.tensor_tensor(qk[:, :, :], qk[:, :, :], qk_parts[:, 0, :, :],
                                       ALU.subtract).then_inc(rest_ready, 1)
                if has("prev", it):
                    low_squares(it, (0,))
                if has("next", it):
                    pool.wait_ge(middle_ready, nxt + 1)
                    pool.tensor_tensor(qk_parts[:, 2, :, :], qk[:, :, :], qk_parts[:, 1, :, :],
                                       ALU.subtract).then_inc(low_part_ready, 1)
                if has("prev", it):
                    low_squares(it, (2, 4, 6))

            iterations(pool, body)

        @block.scalar
        def _(act):
            act.wait_ge(consts_ready, 2)

            def take(name, it, dst, rows_=P, **how):
                take_wait(act, name, it)
                k = BANK_OF[name]
                act.activation(dst, bank[k][0:rows_, 0:dst.shape[-1]], how.pop("func", ACT.Copy),
                               **how).then_inc(drained[k], 1)

            def take_high(name, it, dst, high):
                take_wait(act, name, it)
                act.activation(dst, bank[BANK_OF[name]][:, 0:SP3], ACT.Copy).then_inc(high, 1)

            def take_turned(b, h, u):
                k, n = turn(b, h, u)
                act.wait_ge(turned[k], n)
                act.activation(probsT[0:rows(u), h % RING, u, :], turn_ps[k][0:rows(u), 0:S],
                               ACT.Copy).then_inc(turned_taken[k], 1)

            def exps(b, h):
                for t in range(NT):
                    act.wait_ge(scores_taken, b * (NT * H) + NT * h + t + 1)
                    if t == 0 and not (isinstance(b, int) and b == 0 and h < 2):
                        two = lagged(b, h, 2)
                        for u in (1, 2):
                            k, n = turn(*two, u)
                            act.wait_ge(turned[k], n)
                    act.activation(probs[0:rows(t), h % 2, t, :], nscore[0:rows(t), h % 2, t, :], ACT.Exp,
                                   bias=nmax[0:rows(t), h % 2, t:t + 1], scale=-1.0).then_inc(probs_ready, 1)

            def body(it):
                nxt, prv = it + 1, it - 1
                for s in range(H):
                    two = lagged(it, s, 2)
                    turning = two and (has("own", it) or (s < 2 and it == B))
                    if turning:
                        b2, h2 = two
                        ring_wait(act, it, s)
                        take_turned(b2, h2, 0)
                    if s in SQUARE_SLOTS and has("prev", it):
                        m = SQUARE_SLOTS[s]
                        step_taken(act, f"ffn{m}", it)
                        step_taken(act, f"ffn{m + 1}", it)
                        two_chunks = relu_T[:, m % 4:m % 4 + 2, :]
                        act.activation(two_chunks, two_chunks, ACT.Square).then_inc(squared, 1)
                    if (one := lagged(it, s, 1)) and (has("own", it) or (s < 1 and it == B)):
                        exps(*one)
                    if s % 4 == 3 and (got := lagged(it, s, 7)) and (has("own", it) or (s == 3 and it == B)):
                        b, h = got
                        g = h // 4
                        take_wait(act, f"pv{g}", it)
                        if not (isinstance(b, int) and b == 0 and g == 0):
                            pb, pg = (b, g - 1) if g else (b - 1, 3)
                            take_wait(act, f"otok{pg}", pb + 1 if pg >= 2 else pb)
                        k = BANK_OF[f"pv{g}"]
                        act.activation(oT[:, 0:S], bank[k][:, 0:S], ACT.Copy).then_inc(drained[k], 1)
                    if s == 0 and has("next", it):
                        act.wait_ge(edges_ready, nxt + 1)
                        act.activation(edges[:, :, :, :], edges[:, :, :, :], ACT.Abs).then_inc(edges_abs, 1)
                    if s in ONT_SLOTS and has("prev", it):
                        c = ONT_SLOTS[s]
                        take_high(f"ont{c}", it, o_normT[0][:, c, :], o_normT_high)
                    if s == 5 and has("next", it):
                        for c in range(NC):
                            take_high(f"xt{c}", it, xT[0][:, c, :], xT_high)
                    if s == 9 and has("prev", it):
                        for c in range(NC):
                            take_high(f"x2t{c}", it, x2T[0][:, c, :], x2T_high)
                    if has("next", it):
                        for j in QK_SLOTS.get(s, ()):
                            take(f"qk{j}", it, qk[:, j, :], func=ACT.Identity, bias=bqk_sb[:, j:j + 1],
                                 scale=qscale_sb[:, j:j + 1] if j < NC else 1.0)
                    if s in FFN_SLOTS and has("prev", it):
                        m = FFN_SLOTS[s][0]
                        if not (isinstance(it, int) and it == 1 and m < 4):
                            act.wait_ge(squares_ready, (it - 1) * 4 + m // 2 - 1)
                        take(f"ffn{m}", it, relu_T[:, m % 4, :], func=ACT.Relu)
                    if turning:
                        take_turned(b2, h2, 2)

            act.wait_ge(bias_scaled, 1)
            iterations(act, body)

        @block.vector
        def _(dve):
            steps = [0]

            def step(ins):
                steps[0] += 1
                ins.then_inc(dve_step, 1)
                dve.wait_ge(dve_step, steps[0])

            dve.wait_ge(pool_step, 2)
            step(dve.tensor_copy(dist_f, dist_i))
            step(dve.tensor_scalar(dist[:, :], dist_f, -1.0, None, ALU.mult))
            step(dve.tensor_tensor(dist[:, :], dist_f, dist[:, :], ALU.min))

            def split(parts, src, where):
                step(dve.tensor_copy(parts[0][where], src))
                return dve.tensor_tensor(parts[1][where], src, parts[0][where].bitcast(F32), ALU.subtract)

            dve.wait_ge(weights_loaded, 16 * 12)
            dve.tensor_tensor(bqk_sb[:, 0:NC], bqk_sb[:, 0:NC], qscale_sb[:, :], ALU.mult).then_inc(bias_scaled, 1)
            everything = (slice(None), slice(None), slice(None))
            step(split(wqkv, wqkv_raw, everything))
            step(split(wo, wo_raw, everything))
            for w, n, width, scale, half in ((w1_nat, NM, D, scale1, half1), (w2_nat, NC, HID, scale2, half2)):
                step(dve.tensor_reduce(scale[:, :], w, AX.X, ALU.add, apply_absolute_value=True))
                step(dve.tensor_scalar(scale[:, :], scale[:, :], 1.0 / width, 1e-5, ALU.mult, ALU.max))
                dve.tensor_scalar(half[:, 0, :], scale[:, :], 0.5, None, ALU.mult)
                step(dve.tensor_scalar(half[:, 1, :], scale[:, :], -0.5, None, ALU.mult))
                pos = t_pos.rearrange("p (n w) -> p n w", n=n)
                for i in range(n):
                    neg = t_neg[:, (i % (HID // width)) * width:(i % (HID // width) + 1) * width]
                    dve.tensor_scalar(pos[:, i, :], w[:, i, :], half[:, 0, i:i + 1], None, ALU.is_gt)
                    step(dve.tensor_scalar(neg, w[:, i, :], half[:, 1, i:i + 1], None, ALU.is_lt))
                    step(dve.tensor_tensor(pos[:, i, :] if w is w1_nat else w[:, i, :], pos[:, i, :], neg,
                                           ALU.subtract))
                if w is w1_nat:
                    step(dve.tensor_tensor(pos, pos, w, ALU.subtract))
                    step(dve.tensor_tensor(w, w, pos, ALU.add))
            for c in range(NC):
                last = dve.tensor_copy(scale2_cols[c], scale2[:, c:c + 1].to_broadcast([P, P]))
            last.then_inc(scale2_ready, 1)
            dve.wait_ge(rows_ready, 2)
            dve.wait_ge(filled[0], 1)
            dve.tensor_scalar(low_bv, bank[0][0:RANK, 0:D], gate_bc[0:RANK, :], None,
                              ALU.mult).then_inc(drained[0], 1)
            for m in range(NM):
                k = m % 2
                dve.wait_ge(low_filled, m + 1)
                dve.scalar_tensor_tensor(out=w1_nat[:, m, :], in0=w1_nat[:, m, :], scalar=scale1[:, m:m + 1],
                                         in1=turn_ps[k][:, 0:D], op0=ALU.mult, op1=ALU.add).then_inc(low_ready, 1)
            for n in range(9):
                k, use = SETUP_BANKS[n]
                dve.wait_ge(filled[k], use + 1)
                if n < 4:
                    c, m = n // 2, 4 * (n % 2)
                    last = split(w1T, bank[k][:, :], (slice(None), c, slice(m * P, (m + 4) * P)))
                elif n < 8:
                    m = 2 * (n - 4)
                    last = dve.tensor_copy(w2T[:, m:m + 2, :].rearrange("p m d -> p (m d)"), bank[k][:, :])
                else:
                    last = dve.tensor_copy(scale2_bc[:, :], bank[k][:, 0:D])
                last.then_inc(drained[k], 1)

            def take(name, it, fn):
                take_wait(dve, name, it)
                k = BANK_OF[name]
                fn(bank[k]).then_inc(drained[k], 1)

            def take_low(name, it, parts, c, high, n):
                take_wait(dve, name, it)
                wait_alone(dve, high, n)
                k = BANK_OF[name]
                dve.tensor_tensor(parts[1][:, c, :], bank[k][:, 0:SP3], parts[0][:, c, :].bitcast(F32),
                                  ALU.subtract).then_inc(drained[k], 1)

            def bias_and_max(b, h, tiles):
                for t in tiles:
                    wait_alone(dve, scores_ready, b * (NT * H) + NT * h + t + 1)
                    if t == 0 and not (isinstance(b, int) and b == 0 and h < 2):
                        wait_alone(dve, probs_ready, b * (NT * H) + NT * (h - 1))
                    dve.tensor_tensor_reduce(nscore[0:rows(t), h % 2, t, :],
                                             score_ps[t][0:rows(t), 0:S],
                                             dist[0:rows(t), (2 - t) * P:(2 - t) * P + S],
                                             -slope(h), 3.0e38, ALU.add, ALU.min,
                                             nmax[0:rows(t), h % 2, t:t + 1]).then_inc(scores_taken, 1)

            def layer_norm(k, src, n):
                for t in range(NT):
                    last = dve.bn_stats(stats[:, k, t, :], src[:, t, :])
                last.then_inc(stats_done[k], 1)
                wait_alone(dve, stats_done[k], n + 1)
                for t in range(NT):
                    last = dve.bn_aggr(moments[:, k, t, :], stats[:, k, t, :])
                last.then_inc(moments_done[k], 1)

            def normalize(k, dst, src, n, ready):
                dve.wait_ge(rstd_ready[k], n + 1)
                dve.wait_ge(moments_done[k], n + 1)
                for t in range(NT):
                    last = dve.tensor_scalar(dst[:, t, :], src[:, t, :], moments[:, k, t, 0:1],
                                             rstd[:, k, t:t + 1], ALU.subtract, ALU.mult)
                last.then_inc(ready, 1)

            def take_v(name, it, t, n):
                take(name, it, lambda ps: dve.tensor_tensor(
                    v_sb[:, t:t + n, :, 0:HD],
                    ps[:, 0:n * D].rearrange("p (t h c) -> p t h c", t=n, h=H),
                    bias_bc[:, 0, :].rearrange("p (t h c) -> p t h c", t=1, h=H).to_broadcast([P, n, H, HD]),
                    ALU.add))

            def head_outputs(b, g, it):
                name = f"otok{g}"
                take_wait(dve, name, it)
                k = BANK_OF[name]
                ps = bank[k][:, 0:SP3].rearrange("p (t j c) -> p t j c", t=NT, j=4)
                dve.reciprocal(recip[:, :, :], ps[:, :, :, HD]).then_inc(recip_ready, 1)
                dve.wait_ge(recip_ready, b * 4 + g + 1)
                dve.tensor_tensor(o_norm[:, :, 64 * g:64 * g + 64].rearrange("p t (j c) -> p t j c", j=4),
                                  ps[:, :, :, 0:HD],
                                  recip[:, :, :].rearrange("p t (j c) -> p t j c", c=1).to_broadcast([P, NT, 4, HD]),
                                  ALU.mult).then_inc(drained[k], 1)

            def body(it):
                nxt, prv = it + 1, it - 1
                for s in range(H):
                    if has("own", it):
                        bias_and_max(it, s, (0, 1))
                    if (two := lagged(it, s, 2)) and (has("own", it) or (s < 2 and it == B)):
                        b, h = two
                        ring_wait(dve, it, s)
                        k, n = turn(b, h, 1)
                        dve.wait_ge(turned[k], n)
                        dve.tensor_copy(probsT[0:rows(1), h % RING, 1, :],
                                        turn_ps[k][0:rows(1), 0:S]).then_inc(turned_taken[k], 1)
                    if has("own", it):
                        bias_and_max(it, s, (2,))
                    if s == 0 and has("prev", it):
                        head_outputs(prv, 2, it)
                    if s == 2 and has("next", it):
                        dve.wait_ge(tokens_ready, nxt + 1)
                        layer_norm(0, h_new, nxt)
                    if s == 3 and has("next", it):
                        normalize(0, xn, h_new, nxt, xn_ready)
                    if s == 4:
                        if has("prev", it):
                            head_outputs(prv, 3, it)
                        if has("own", it):
                            take_v("v01", it, 0, 2)
                    if s == 5 and has("own", it):
                        take_v("v2", it, 2, 1)
                    if s in ONT_SLOTS and has("prev", it):
                        c = ONT_SLOTS[s]
                        take_low(f"ont{c}", it, o_normT, c, o_normT_high, prv * NC + c + 1)
                    if s == 5 and has("next", it):
                        for c in range(NC):
                            take_low(f"xt{c}", it, xT, c, xT_high, nxt * NC + c + 1)
                    if s == 9 and has("prev", it):
                        for c in range(NC):
                            take_low(f"x2t{c}", it, x2T, c, x2T_high, prv * NC + c + 1)
                    if s == 9 and has("own", it):
                        head_outputs(it, 0, it)
                    if s == 6 and has("prev", it):
                        dve.wait_ge(h_old_loaded, it * 16)
                        if has("late", it):
                            dve.wait_ge(y_summed, it - 1)
                        take("proj0", it, lambda ps: dve.tensor_tensor(
                            h_mid[:, 0:2, :].rearrange("p t d -> p (t d)"), ps[:, :],
                            h_old[:, 0:2, :].rearrange("p t d -> p (t d)"), ALU.add))
                        take("proj1", it, lambda ps: dve.tensor_tensor(h_mid[:, 2, :], ps[:, 0:D],
                                                                       h_old[:, 2, :], ALU.add))
                    if s == 7 and has("prev", it):
                        step_taken(dve, "proj1", it)
                        layer_norm(1, h_mid, prv)
                    if s == 8 and has("prev", it):
                        dve.wait_ge(stored, it * 32)
                        normalize(1, x2, h_mid, prv, x2_ready)
                    if s == 11:
                        if has("next", it):
                            for j in range(NQ):
                                step_taken(dve, f"qk{j}", it)
                            dve.tensor_copy(qk_parts[:, 0, :, :], qk[:, :, :]).then_inc(high_ready, 1)
                    if s == 12 and has("own", it):
                        head_outputs(it, 1, it)
                    if s in FFN_SLOTS and has("prev", it):
                        m = FFN_SLOTS[s][1]
                        if not (isinstance(it, int) and it == 1 and m < 4):
                            dve.wait_ge(squares_ready, (it - 1) * 4 + m // 2 - 1)
                        take(f"ffn{m}", it, lambda ps: dve.tensor_scalar(relu_T[:, m % 4, :], ps[:, 0:S], 0.0, None,
                                                                         ALU.max))
                    if s in SQUARE_SLOTS and has("prev", it):
                        m = SQUARE_SLOTS[s]
                        dve.wait_ge(squared, prv * 4 + m // 2 + 1)
                        dve.tensor_copy(act_T[0][:, m:m + 2, :], relu_T[:, m % 4:m % 4 + 2, :]).then_inc(
                            square_high, 1)
                    if s == 12 and has("next", it):
                        dve.wait_ge(rest_ready, nxt + 1)
                        dve.tensor_copy(qk_parts[:, 1, :, :], qk[:, :, :]).then_inc(middle_ready, 1)
                    if s in Y_SLOTS and has("late", it):
                        t = Y_SLOTS[s]
                        take(f"y{t}", it, lambda ps: dve.tensor_tensor(
                            y_sb[0:rows(t), t, :], ps[0:rows(t), 0:D], scale2_bc[0:rows(t), :], ALU.mult))

            iterations(dve, body)

        @block.tensor
        def _(pe):
            pe.wait_ge(consts_ready, 2)
            pe.wait_ge(weights_loaded, 16 * 12)
            pe.matmul(bank[0][0:RANK, 0:D], low_bT, low_v, start=True, stop=True).then_inc(filled[0], 1)
            pe.wait_ge(drained[0], 1)
            for m in range(NM):
                k = m % 2
                if m >= 2:
                    pe.wait_ge(low_ready, m - 1)
                pe.matmul(turn_ps[k][:, 0:D], low_uT[:, m * P:(m + 1) * P], low_bv, start=True,
                          stop=True).then_inc(low_filled, 1)
            pe.wait_ge(low_ready, NM)
            pe.wait_ge(scale2_ready, 1)
            for n in range(9):
                k, use = SETUP_BANKS[n]
                if use:
                    pe.wait_ge(drained[k], use)
                if n == 8:
                    for c in range(NC):
                        last = pe.matmul(bank[k][:, c * P:(c + 1) * P], scale2_cols[c], ident[:, :],
                                         start=True, stop=True)
                    last.then_inc(filled[k], 1)
                    break
                for i in range(4):
                    if n < 4:
                        src = w1_nat[:, 4 * (n % 2) + i, (n // 2) * P:(n // 2 + 1) * P]
                    else:
                        m, c = 2 * (n - 4) + i // 2, i % 2
                        src = w2_nat[:, c, m * P:(m + 1) * P]
                    last = pe.transpose(bank[k][:, i * P:(i + 1) * P], src, ident[:, :])
                last.then_inc(filled[k], 1)

            def scores(b, h):
                for half in range(2):
                    if h == HALF * half:
                        pe.wait_ge(aug_loaded[half], b * 192 + 192)
                for t in range(NT):
                    n = NT * h + t
                    if not (isinstance(b, int) and b == 0 and h == 0):
                        pe.wait_ge(scores_taken, b * (NT * H) + n - 2)
                    pe.matmul(score_ps[t][0:rows(t), 0:S], q_aug[:, h, t * P:t * P + rows(t)], k_aug[:, h, :],
                              start=True, stop=True).then_inc(scores_ready, 1)

            def transpose_probs(b, h, tiles):
                pe.wait_ge(probs_ready, b * (NT * H) + NT * (h + 1))
                for u in tiles:
                    k, n = turn(b, h, u)
                    if not (isinstance(b, int) and b == 0 and NT * h + u < 2):
                        pe.wait_ge(turned_taken[k], n - 1)
                    for t in range(NT):
                        last = pe.transpose(turn_ps[k][0:rows(u), t * P:t * P + rows(t)],
                                            probs[0:rows(t), h % 2, t, u * P:u * P + rows(u)],
                                            ident[0:rows(t), 0:rows(t)])
                    last.then_inc(turned[k], 1)

            def times_v(b, g, it):
                for k in range(2):
                    pe.wait_ge(turned_taken[k], b * (NT * H // 2) + 6 * (g + 1))
                name = f"pv{g}"
                if g == 0:
                    for v_name in ("v01", "v2"):
                        step_taken(pe, v_name, it)
                fill_wait(pe, name, it)
                k = BANK_OF[name]
                for u in range(NT):
                    for j in range(4):
                        h = 4 * g + j
                        last = pe.matmul(bank[k][32 * j:32 * j + 32, 0:S], v_sb[0:rows(u), u, h, :],
                                         probsT[0:rows(u), h % RING, u, :], start=(u == 0), stop=(u == NT - 1))
                last.then_inc(filled[k], 1)

            def fill(name, it, fn):
                fill_wait(pe, name, it)
                k = BANK_OF[name]
                fn(bank[k]).then_inc(filled[k], 1)

            def transpose_rows(src, c):
                def fn(ps):
                    for t in range(NT):
                        last = pe.transpose(ps[:, t * P:(t + 1) * P], src[:, t, c * P:(c + 1) * P], ident[:, :])
                    return last
                return fn

            def split_product(dst, lhs, rhs, n=NC, products=((0, 0), (0, 1), (1, 0))):
                for c in range(n):
                    for a, b in products:
                        last = pe.matmul(dst, lhs(a, c), rhs(b, c), start=(c == 0 and (a, b) == products[0]),
                                         stop=(c == n - 1 and (a, b) == products[-1]))
                return last

            def head_outputs(b, g, it):
                step_taken(pe, f"pv{g}", it, back=int(g == 2))

                def fn(ps):
                    for t in range(NT):
                        last = pe.transpose(ps[:, t * P:(t + 1) * P], oT[:, t * P:(t + 1) * P], ident[:, :])
                    return last
                fill(f"otok{g}", it, fn)

            def v_rows(ps, tiles):
                for i, t in enumerate(tiles):
                    last = split_product(ps[:, i * D:(i + 1) * D],
                                         lambda a, c: xT[a][:, c, t * P:(t + 1) * P],
                                         lambda b, c: wqkv[b][:, c, 2 * D:3 * D])
                return last

            def body(it):
                nxt, prv = it + 1, it - 1
                for s in range(H):
                    if has("own", it):
                        scores(it, s)
                    two = lagged(it, s, 2)
                    turning = two and (has("own", it) or (s < 2 and it == B))
                    if turning:
                        transpose_probs(*two, (0, 1))
                    if s % 4 == 3 and (got := lagged(it, s, 7)) and (has("own", it) or (s == 3 and it == B)):
                        times_v(got[0], got[1] // 4, it)
                    if s == 0 and has("prev", it):
                        head_outputs(prv, 2, it)
                    if s == 5 and has("own", it):
                        fill("v2", it, lambda ps: v_rows(ps, (2,)))
                    if s in ONT_SLOTS and has("prev", it):
                        c = ONT_SLOTS[s]
                        step_taken(pe, "otok3" if c else "otok2", it)
                        fill(f"ont{c}", it, transpose_rows(o_norm, c))
                    if s in Y_SLOTS and has("late", it):
                        t = Y_SLOTS[s]
                        pe.wait_ge(squares_ready, (it - 1) * (NM // 2))
                        fill(f"y{t}", it, lambda ps: split_product(
                            ps[0:rows(t), 0:D], lambda a, m: act_T[a][:, m, t * P:t * P + rows(t)],
                            lambda b, m: w2T[:, m, :], n=NM, products=((0, 0), (1, 0))))
                    if s == 4:
                        if has("prev", it):
                            head_outputs(prv, 3, it)
                        if has("own", it):
                            fill("v01", it, lambda ps: v_rows(ps, (0, 1)))
                    if s == 5:
                        if has("next", it):
                            pe.wait_ge(xn_ready, nxt + 1)
                            for c in range(NC):
                                fill(f"xt{c}", it, transpose_rows(xn, c))
                    if s == 9 and has("prev", it):
                        pe.wait_ge(x2_ready, it)
                        for c in range(NC):
                            fill(f"x2t{c}", it, transpose_rows(x2, c))
                    if has("next", it):
                        for j in QK_SLOTS.get(s, ()):
                            if j == 0:
                                for c in range(NC):
                                    step_taken(pe, f"xt{c}", it)
                            fill(f"qk{j}", it, lambda ps: split_product(
                                ps[:, 0:SE], lambda a, c: wqkv[a][:, c, j * P:(j + 1) * P],
                                lambda b, c: xT[b][:, c, 0:SE]))
                    if s == 9 and has("own", it):
                        head_outputs(it, 0, it)
                    if s == 6 and has("prev", it):
                        for c in range(NC):
                            step_taken(pe, f"ont{c}", it)

                        def proj(ps, tiles):
                            for i, t in enumerate(tiles):
                                last = split_product(ps[:, i * D:(i + 1) * D],
                                                     lambda a, c: o_normT[a][:, c, t * P:(t + 1) * P],
                                                     lambda b, c: wo[b][:, c, :])
                            return last
                        fill("proj0", it, lambda ps: proj(ps, (0, 1)))
                        fill("proj1", it, lambda ps: proj(ps, (2,)))
                    if s == 12 and has("own", it):
                        head_outputs(it, 1, it)
                    if s in FFN_SLOTS and has("prev", it):
                        if s == min(FFN_SLOTS):
                            for c in range(NC):
                                step_taken(pe, f"x2t{c}", it)
                        for m in FFN_SLOTS[s]:
                            fill(f"ffn{m}", it, lambda ps: split_product(
                                ps[:, 0:SE], lambda a, c: w1T[a][:, c, m * P:(m + 1) * P],
                                lambda b, c: x2T[b][:, c, 0:SE]))
                    if turning:
                        transpose_probs(*two, (2,))

            iterations(pe, body)


def kernel(**inputs):
    import concourse.bacc as bacc
    from concourse.bass_utils import run_bass_kernel_spmd

    a = {n: np.asarray(v) for n, v in inputs.items()}
    order = np.arange(2 * D).reshape(NQ, HALF, HD).transpose(0, 2, 1).reshape(-1)
    order = np.concatenate([order, np.arange(2 * D, 3 * D)])
    arrays = {
        "x_dram": a["x"],
        "txt_dram": a["txt"],
        "wqkvT_dram": np.ascontiguousarray(a["L0_attn_W_qkv"][order].T),
        "bqk_dram": np.ascontiguousarray(a["L0_attn_b_qkv"][order[:2 * D]].reshape(NQ, P).T),
        "q_scale_dram": np.array([[HD ** -0.5 / 2.0 ** (-8.0 * (HALF * j + p % HALF) / H) for j in range(NC)]
                                  for p in range(P)], np.float32),
        "bv_dram": np.ascontiguousarray(a["L0_attn_b_qkv"][2 * D:].reshape(1, D)),
        "woT_dram": np.ascontiguousarray(a["L0_attn_W_out"].T),
        "bo_dram": np.ascontiguousarray(a["L0_attn_b_out"].reshape(1, D)),
        "fast_bT_dram": np.ascontiguousarray(a["L0_ffn_fast_b"].T),
        "w_fc_dram": a["L0_ffn_w_fc"],
        "w_proj_dram": a["L0_ffn_w_proj"],
        "uT_dram": np.ascontiguousarray(a["L0_ffn_u"].T),
        "v_dram": a["L0_ffn_v"],
        "gate_dram": np.ascontiguousarray(a["L0_ffn_gate"].reshape(1, 1)),
    }
    nc = bacc.Bacc("TRN2", target_bir_lowering=False, num_devices=1)
    args = [nc.dram_tensor(n, v.shape, mybir.dt.from_np(v.dtype), kind="ExternalInput").ap()
            for n, v in arrays.items()]
    out = nc.dram_tensor("out_dram", (B, S, D), F32, kind="ExternalOutput").ap()
    early_fusion_kernel(nc, *args, out)
    return run_bass_kernel_spmd(nc, [arrays], core_ids=[0]).results[0]["out_dram"]
```

```python
from contextlib import ExitStack

import numpy as np

import concourse.bass as bass
from concourse import mybir

F32 = mybir.dt.float32
BF16 = mybir.dt.bfloat16
F32R = mybir.dt.float32r
I32 = mybir.dt.int32
ALU = mybir.AluOpType
ACT = mybir.ActivationFunctionType
AX = mybir.AxisListType

B, IMG, TXT, D = 32, 256, 77, 256
S = IMG + TXT
P = 128
ROWS = [P, P, S - 2 * P]
NT = len(ROWS)
SP3 = NT * P
H, HD = 16, 16
HID, RANK = 1024, 16
NC = D // P
NM = HID // P
HALF = H // 2
EPS = 1e-5
Q_PARTS = [0, 0, 1, 1, 0, 2]
K_PARTS = [0, 1, 0, 1, 2, 0]
KAUG = HD * len(Q_PARTS)
RING = 8
NQ = 2 * NC
SE = S + 1
BW = S + 2 * P
QK_SLOTS = {6: (0,), 8: (1, 2), 9: (3,)}
FFN_SLOTS = {10: (0, 1), 12: (2, 3), 13: (4, 5), 14: (6, 7)}
SQUARE_SLOTS = {11: 0, 13: 2, 14: 4, 15: 6}
ONT_SLOTS = {1: 0, 5: 1}
Y_SLOTS = {0: 0, 1: 1, 2: 2}

USES = [
    ("otok2", "prev"), ("y0", "late"), ("low_bv", "weights"),
    ("ont0", "prev"), ("y1", "late"), ("low01", "weights"),
    ("y2", "late"), ("low23", "weights"),
    ("pv3", "prev"), ("low45", "weights"),
    ("otok3", "prev"), ("v01", "own"), ("low67", "weights"),
    ("v2", "own"), ("ont1", "prev"), ("xt0", "next"), ("xt1", "next"),
    ("qk0", "next"), ("proj0", "prev"), ("proj1", "prev"), ("w1t0", "weights"),
    ("pv0", "own"), ("w1t1", "weights"),
    ("qk1", "next"), ("qk2", "next"), ("w1t2", "weights"),
    ("x2t0", "prev"), ("x2t1", "prev"), ("qk3", "next"), ("w1t3", "weights"),
    ("otok0", "own"), ("ffn0", "prev"), ("ffn1", "prev"),
    ("pv1", "own"), ("scale2", "weights"),
    ("otok1", "own"), ("ffn2", "prev"), ("ffn3", "prev"),
    ("ffn4", "prev"), ("ffn5", "prev"),
    ("ffn6", "prev"), ("ffn7", "prev"), ("w2t0", "weights"), ("w2t1", "weights"),
    ("pv2", "own"), ("w2t2", "weights"), ("w2t3", "weights"),
]
BANKS = 3
EVERY = [name for name, part in USES if part != "weights"]
ONCE = [name for name, part in USES if part == "weights"]
BANK_OF = {name: i % BANKS for names in (EVERY, ONCE) for i, name in enumerate(names)}
assert len(EVERY) % BANKS == 0
LOOP_FIRST, LOOP_END = 2, B - 2


def parts_of(it):
    if not isinstance(it, int):
        return ("own", "prev", "late", "next", "load")
    here = (("own", 0 <= it < B), ("prev", 1 <= it <= B), ("late", 2 <= it <= B + 1), ("next", it < B - 1),
            ("load", it < B - 2), ("weights", it == 0))
    return tuple(p for p, on in here if on)


def uses_in(k, it, before=None):
    n = 0
    for name, part in USES:
        if name == before:
            break
        n += BANK_OF[name] == k and part in parts_of(it)
    return n


def bank_uses_before(name, it, back=0):
    if back and isinstance(it, int):
        return bank_uses_before(name, it - 1)
    k = BANK_OF[name]
    whole = it if isinstance(it, int) else LOOP_FIRST
    n = sum(uses_in(k, i) for i in range(-1, whole)) + uses_in(k, it, before=name)
    if isinstance(it, int):
        return n
    return (it - LOOP_FIRST) * uses_in(k, it) + n - back * uses_in(k, it)


def early_fusion_kernel(nc, x, txt, wqkvT, bqk, q_scale, bv, woT, bo, fast_bT, w_fc, w_proj, uT, v, gate, out):
    ctx = ExitStack()
    with ctx:
        def sb(name, shape, dt=F32):
            return ctx.enter_context(nc.sbuf_tensor(name, shape, dt))

        def psum(name):
            return ctx.enter_context(nc.psum_tensor(name, [P, 512], F32))

        def sem(name):
            return ctx.enter_context(nc.semaphore(name))

        def pair(name, shape):
            return [sb(f"{name}_{part}", shape, F32R) for part in ("high", "low")]

        wqkv = pair("wqkv", [P, NC, 3 * D])
        wo = pair("wo", [P, NC, D])
        w1T = pair("w1T", [P, NC, HID])
        w2T = sb("w2T", [P, NM, D], F32R)
        scale2_bc = sb("scale2_bc", [P, D])
        qscale_sb = sb("qscale_sb", [P, NC])
        bqk_sb = sb("bqk_sb", [P, NQ])
        bias_bc = sb("bias_bc", [P, 2, D])
        ident = sb("ident", [P, P])
        dist = sb("dist", [P, BW])
        mhalf = sb("mhalf", [P, NT])

        imgA = sb("imgA", [P, 2, IMG + 1])
        imgB = sb("imgB", [P, 2, IMG + 1])
        edges = sb("edges", [P, 2, 2, IMG])
        h_new = sb("h_new", [P, NT, D])
        h_bias = sb("h_bias", [P, NT, D])
        h_old = sb("h_old", [P, NT, D])
        stats = sb("stats", [P, 2, NT, 6])
        moments = sb("moments", [P, 2, NT, 2])
        var_eps = sb("var_eps", [P, 2, NT])
        rstd = sb("rstd", [P, 2, NT])
        xn = sb("xn", [P, NT, D])
        xT = pair("xT", [P, NC, SP3])
        qk = sb("qk", [P, NQ, S])
        qk_parts = sb("qk_parts", [P, 3, NQ, S], BF16)
        q_aug = sb("q_aug", [KAUG, H, S], BF16)
        k_aug = sb("k_aug", [KAUG, H, S], BF16)

        v_sb = sb("v_sb", [P, NT, H, 32])
        nscore = sb("nscore", [P, 2, NT, S])
        nmax = sb("nmax", [P, 2, NT])
        probs = sb("probs", [P, 2, NT, S])
        probsT = sb("probsT", [P, RING, NT, S])
        oT = sb("oT", [P, SP3])
        recip = sb("recip", [P, NT, 4])
        o_norm = sb("o_norm", [P, NT, D])

        o_normT = pair("o_normT", [P, NC, SP3])
        h_mid = sb("h_mid", [P, NT, D])
        x2 = sb("x2", [P, NT, D])
        x2T = pair("x2T", [P, NC, SP3])
        relu_T = sb("relu_T", [P, 4, S])
        with ExitStack() as scratch:
            def early(name, shape):
                return scratch.enter_context(nc.sbuf_tensor(name, shape, F32))

            w1_nat = early("w1_nat", [P, NM, D])
            w2_nat = early("w2_nat", [P, NC, HID])
            scale2_cols = early("scale2_cols", [P, NC, P])
            low_bv = early("low_bv", [RANK, D])
            bias_row = early("bias_row", [1, 2 * D + 1])
        act_T = pair("act_T", [P, NM, S])
        y_sb = x2

        flat = probsT[:, :, :, :].rearrange("p r t s -> p (r t s)")
        wqkv_raw = flat[:, 0:NC * 3 * D].rearrange("p (c n) -> p c n", c=NC)
        wo_raw = flat[:, NC * 3 * D:NC * 4 * D].rearrange("p (c n) -> p c n", c=NC)
        nscore_flat = nscore[:, :, :, :].rearrange("p r t s -> p (r t s)")
        dist_i = nscore_flat[:, 0:BW].bitcast(I32)
        dist_f = nscore_flat[:, BW:2 * BW]

        relu_flat = relu_T[:, :, :].rearrange("p a b -> p (a b)")
        ternary = relu_flat[:, 0:HID]
        low_v = relu_flat[0:RANK, HID:HID + D]
        low_bT = relu_flat[0:RANK, HID + D:HID + D + RANK]
        low_uT = [t[0:RANK, :, :].rearrange("p a b -> p (a b)")[:, 0:HID // 2] for t in (x2, h_mid)]
        gate_bc = sb("gate_bc", [P, 1])
        scale1 = sb("scale1", [P, NM])
        half1 = sb("half1", [P, 2, NM])
        scale2 = sb("scale2", [P, NC])
        half2 = sb("half2", [P, 2, NC])

        score_ps = [psum(f"score_ps{t}") for t in range(NT)]
        turn_ps = [psum("turn_ps0"), psum("turn_ps1")]
        bank = [psum(f"bank{k}") for k in range(BANKS)]

        waits_met = sem("waits_met")
        qkv_loaded = sem("qkv_loaded")
        ffn_loaded = sem("ffn_loaded")
        pool_step = sem("pool_step")
        consts_ready = sem("consts_ready")
        rows_ready = sem("rows_ready")
        dve_step = sem("dve_step")
        w2_ready = sem("w2_ready")
        bias_scaled = sem("bias_scaled")
        scale2_ready = sem("scale2_ready")
        filled = [sem(f"bank_filled{k}") for k in range(BANKS)]
        drained = [sem(f"bank_drained{k}") for k in range(BANKS)]
        tokens_loaded = sem("tokens_loaded")
        edges_ready = sem("edges_ready")
        edges_abs = sem("edges_abs")
        edges_sum = sem("edges_sum")
        tokens_ready = sem("tokens_ready")
        stats_done = [sem("stats1_done"), sem("stats2_done")]
        moments_done = [sem("moments1_done"), sem("moments2_done")]
        eps_added = [sem("eps1_added"), sem("eps2_added")]
        rstd_ready = [sem("rstd1_ready"), sem("rstd2_ready")]
        xn_ready = sem("xn_ready")
        x2_ready = sem("x2_ready")
        h_bias_ready = sem("h_bias_ready")
        h_old_loaded = sem("h_old_loaded")
        xT_high = sem("xT_high")
        high_ready = sem("high_ready")
        rest_ready = sem("rest_ready")
        middle_ready = sem("middle_ready")
        low_part_ready = sem("low_part_ready")
        aug_loaded = [sem("aug_loaded0"), sem("aug_loaded1")]
        scores_ready = sem("scores_ready")
        scores_taken = sem("scores_taken")
        probs_ready = sem("probs_ready")
        turned = [sem("turned0"), sem("turned1")]
        turned_taken = [sem("turned_taken0"), sem("turned_taken1")]
        recip_ready = sem("recip_ready")
        o_normT_high = sem("o_normT_high")
        x2T_high = sem("x2T_high")
        squared = sem("squared")
        square_high = sem("square_high")
        y_summed = sem("y_summed")
        squares_ready = sem("squares_ready")
        stored = sem("stored")

        def fill_wait(eng, name, it):
            n = bank_uses_before(name, it)
            if not (isinstance(n, int) and n == 0):
                eng.wait_ge(drained[BANK_OF[name]], n)

        def take_wait(eng, name, it, back=0):
            eng.wait_ge(filled[BANK_OF[name]], bank_uses_before(name, it, back) + 1)

        def wait_alone(eng, semaphore, value):
            eng.wait_ge(semaphore, value)
            if not isinstance(value, int):
                eng.sem_inc(waits_met, 1)

        def step_taken(eng, name, it, back=0):
            wait_alone(eng, drained[BANK_OF[name]], bank_uses_before(name, it, back) + 1)

        def ring_wait(eng, it, s):
            group = (s - 2) // 4 - RING // 4
            back = int(group < -1)
            if not (isinstance(it, int) and it - back < (1 if group % 4 == 3 else 0)):
                take_wait(eng, f"pv{group % 4}", it, back)

        def rows(t):
            return ROWS[t]

        def slope(h):
            return float(np.power(np.float32(2.0), np.float32(-8.0 * h / H)))

        def lagged(b, s, lag):
            if s >= lag:
                return b, s - lag
            if isinstance(b, int) and b == 0:
                return None
            return b - 1, s - lag + H

        def turn(b, h, u):
            m = NT * h + u
            return m % 2, b * (NT * H // 2) + m // 2 + 1

        def iterations(eng, body):
            for it in range(-1, LOOP_FIRST):
                body(it)
            with eng.Fori(LOOP_FIRST, LOOP_END) as it:
                body(it)
            for it in range(LOOP_END, B + 2):
                body(it)

        def has(part, it):
            return part in parts_of(it)

        block = ctx.enter_context(nc.Block())

        @block.sync
        def _(sp):
            qkv_loads = [
                (wqkv_raw, wqkvT.rearrange("(c p) n -> p c n", p=P)),
                (bqk_sb[:, :], bqk), (qscale_sb[:, :], q_scale),
                (bias_row[:, 0:D], bv), (bias_row[:, D:2 * D], bo), (bias_row[:, 2 * D:2 * D + 1], gate),
                (wo_raw, woT.rearrange("(c p) n -> p c n", p=P)),
            ]
            ffn_loads = [
                (w1_nat[:, :, :], w_fc.rearrange("(m p) d -> p m d", p=P)),
                (w2_nat[:, :, :], w_proj.rearrange("(c p) m -> p c m", p=P)),
                (low_uT[0], uT[:, 0:HID // 2]), (low_uT[1], uT[:, HID // 2:HID]), (low_v, v), (low_bT, fast_bT),
            ]
            sp.sem_inc(stored, 32)

            def load_tokens(n):
                img = x[n, 0]
                sp.dma_start(imgA[:, :, 0:IMG], img.rearrange("(t p) c -> p t c", p=P)).then_inc(tokens_loaded, 16)
                sp.dma_start(imgB[:, 0, 0:IMG], img[1:P + 1, :]).then_inc(tokens_loaded, 16)
                sp.dma_start(imgB[0:112, 1, 0:IMG], img[P + 1:P + 113, :]).then_inc(tokens_loaded, 16)
                sp.dma_start(imgB[112:127, 1, 0:IMG], img[P + 113:IMG, :]).then_inc(tokens_loaded, 16)
                sp.dma_start(h_new[0:TXT, 2, :], txt[n]).then_inc(tokens_loaded, 16)

            def load_aug(half, parts=range(3)):
                for part in parts:
                    for aug, used, block_ in ((q_aug, Q_PARTS, half), (k_aug, K_PARTS, 2 + half)):
                        for i in (i for i, p in enumerate(used) if p == part):
                            sp.dma_start(aug[HD * i:HD * (i + 1), HALF * half:HALF * (half + 1), :],
                                         qk_parts[:, part, block_, :]).then_inc(aug_loaded[half], 16)

            def body(it):
                if isinstance(it, int) and it == -1:
                    for dst, src in qkv_loads:
                        sp.dma_start(dst, src).then_inc(qkv_loaded, 16)
                    sp.wait_ge(consts_ready, 1)
                    load_tokens(0)
                    for dst, src in ffn_loads:
                        sp.dma_start(dst, src).then_inc(ffn_loaded, 16)
                if has("late", it):
                    wait_alone(sp, y_summed, it - 1)
                    sp.dma_start(out[it - 2, 0:2 * P, :].rearrange("(t p) d -> p t d", p=P),
                                 y_sb[:, 0:2, :]).then_inc(stored, 16)
                    sp.dma_start(out[it - 2, 2 * P:S, :], y_sb[0:TXT, 2, :]).then_inc(stored, 16)
                if has("own", it):
                    wait_alone(sp, h_bias_ready, it + 1)
                    if has("prev", it):
                        step_taken(sp, "proj1", it)
                    sp.dma_start(h_old[:, :, :], h_bias[:, :, :]).then_inc(h_old_loaded, 16)
                if has("load", it):
                    wait_alone(sp, xn_ready, it + 2)
                    wait_alone(sp, h_bias_ready, it + 2)
                    load_tokens(it + 2)
                if has("next", it):
                    if has("own", it):
                        wait_alone(sp, scores_ready, it * (NT * H) + NT * HALF)
                    for part, ready in enumerate((high_ready, middle_ready, low_part_ready)):
                        wait_alone(sp, ready, it + 2)
                        load_aug(0, (part,))
                    if has("own", it):
                        wait_alone(sp, scores_ready, it * (NT * H) + NT * H)
                    load_aug(1)

            iterations(sp, body)
            sp.wait_ge(stored, 32 * (B + 1))

        @block.gpsimd
        def _(pool):
            pool.iota(dist_i, pattern=[[1, BW]], base=-2 * P, channel_multiplier=-1).then_inc(pool_step, 1)
            pool.memset(imgA[:, :, :], 0.0)
            pool.memset(imgB[:, :, :], 0.0)
            pool.memset(h_new[:, :, :], 0.0).then_inc(consts_ready, 1)
            pool.memset(mhalf[:, :], -0.5)
            pool.memset(ident[:, :], 0.0).then_inc(pool_step, 1)
            pool.memset(oT[:, :], 1.0)
            pool.memset(v_sb[:, :, :, HD:HD + 1], 1.0)
            pool.memset(v_sb[:, :, :, HD + 1:32], 0.0)
            pool.wait_ge(pool_step, 2)
            pool.affine_select(out=ident[:, :], in_=ident[:, :], compare_op=ALU.not_equal, fill=1.0,
                               base=0, pattern=[[-1, P]], channel_multiplier=1).then_inc(consts_ready, 1)
            pool.wait_ge(qkv_loaded, 16 * 7)
            pool.partition_broadcast(bias_bc[:, :, :].rearrange("p a d -> p (a d)"), bias_row[:, 0:2 * D],
                                     channels=P).then_inc(rows_ready, 1)
            pool.partition_broadcast(gate_bc[:, :], bias_row[:, 2 * D:2 * D + 1], channels=P).then_inc(rows_ready, 1)
            pool.wait_ge(rows_ready, 2)

            def make_rstd(k, n):
                wait_alone(pool, moments_done[k], n + 1)
                pool.tensor_scalar(var_eps[:, k, :], moments[:, k, :, 1], EPS, None, ALU.add).then_inc(eps_added[k], 1)
                pool.wait_ge(eps_added[k], n + 1)
                pool.tensor_tensor(rstd[:, k, :], var_eps[:, k, :], mhalf[:, :], ALU.pow).then_inc(rstd_ready[k], 1)

            def low_squares(it, chunks):
                for m in chunks:
                    pool.wait_ge(square_high, (it - 1) * 4 + m // 2 + 1)
                    pool.tensor_tensor(act_T[1][:, m:m + 2, :], relu_T[:, m % 4:m % 4 + 2, :],
                                       act_T[0][:, m:m + 2, :].bitcast(F32), ALU.subtract).then_inc(squares_ready, 1)

            def differences(n):
                pool.wait_ge(tokens_loaded, n * 80 + 80)
                pool.tensor_tensor(edges[:, 0, :, :], imgA[:, :, 0:IMG], imgB[:, :, 1:IMG + 1], ALU.subtract)
                pool.tensor_tensor(edges[:, 1, :, :], imgB[:, :, 0:IMG], imgA[:, :, 1:IMG + 1],
                                   ALU.subtract).then_inc(edges_ready, 1)

            def body(it):
                nxt = it + 1
                if isinstance(it, int) and it == -1:
                    differences(0)
                if has("next", it):
                    pool.wait_ge(edges_abs, nxt + 1)
                    pool.tensor_tensor(edges[:, 0, :, :], edges[:, 0, :, :], edges[:, 1, :, :],
                                       ALU.add).then_inc(edges_sum, 1)
                    wait_alone(pool, edges_sum, nxt + 1)
                    pool.tensor_scalar(h_new[:, 0:2, :], edges[:, 0, :, :], 0.0, 1.0, ALU.max,
                                       ALU.min).then_inc(tokens_ready, 1)
                if has("next", it):
                    make_rstd(0, nxt)
                if has("late", it):
                    for t in range(NT):
                        step_taken(pool, f"y{t}", it)
                    pool.tensor_tensor(y_sb[:, :, :], y_sb[:, :, :], h_mid[:, :, :], ALU.add).then_inc(y_summed, 1)
                if has("prev", it):
                    make_rstd(1, it - 1)
                if has("next", it):
                    if has("own", it):
                        pool.wait_ge(h_old_loaded, it * 16 + 16)
                    pool.tensor_tensor(h_bias[:, :, :], h_new[:, :, :],
                                       bias_bc[:, 1:2, :].to_broadcast([P, NT, D]),
                                       ALU.add).then_inc(h_bias_ready, 1)
                if has("load", it):
                    differences(it + 2)
                if has("next", it):
                    pool.wait_ge(high_ready, nxt + 1)
                    pool.tensor_tensor(qk[:, :, :], qk[:, :, :], qk_parts[:, 0, :, :],
                                       ALU.subtract).then_inc(rest_ready, 1)
                if has("prev", it):
                    low_squares(it, (0,))
                if has("next", it):
                    pool.wait_ge(middle_ready, nxt + 1)
                    pool.tensor_tensor(qk_parts[:, 2, :, :], qk[:, :, :], qk_parts[:, 1, :, :],
                                       ALU.subtract).then_inc(low_part_ready, 1)
                if has("prev", it):
                    low_squares(it, (2, 4, 6))

            iterations(pool, body)

        @block.scalar
        def _(act):
            act.wait_ge(consts_ready, 2)

            def take(name, it, dst, rows_=P, **how):
                take_wait(act, name, it)
                k = BANK_OF[name]
                act.activation(dst, bank[k][0:rows_, 0:dst.shape[-1]], how.pop("func", ACT.Copy),
                               **how).then_inc(drained[k], 1)

            def take_high(name, it, dst, high):
                take_wait(act, name, it)
                act.activation(dst, bank[BANK_OF[name]][:, 0:SP3], ACT.Copy).then_inc(high, 1)

            def take_turned(b, h, u):
                k, n = turn(b, h, u)
                act.wait_ge(turned[k], n)
                act.activation(probsT[0:rows(u), h % RING, u, :], turn_ps[k][0:rows(u), 0:S],
                               ACT.Copy).then_inc(turned_taken[k], 1)

            def exps(b, h):
                for t in range(NT):
                    act.wait_ge(scores_taken, b * (NT * H) + NT * h + t + 1)
                    if t == 0 and not (isinstance(b, int) and b == 0 and h < 2):
                        two = lagged(b, h, 2)
                        for u in (1, 2):
                            k, n = turn(*two, u)
                            act.wait_ge(turned[k], n)
                    act.activation(probs[0:rows(t), h % 2, t, :], nscore[0:rows(t), h % 2, t, :], ACT.Exp,
                                   bias=nmax[0:rows(t), h % 2, t:t + 1], scale=-1.0).then_inc(probs_ready, 1)

            def body(it):
                nxt, prv = it + 1, it - 1
                for s in range(H):
                    two = lagged(it, s, 2)
                    turning = two and (has("own", it) or (s < 2 and it == B))
                    if turning:
                        b2, h2 = two
                        ring_wait(act, it, s)
                        take_turned(b2, h2, 0)
                    if s in SQUARE_SLOTS and has("prev", it):
                        m = SQUARE_SLOTS[s]
                        step_taken(act, f"ffn{m}", it)
                        step_taken(act, f"ffn{m + 1}", it)
                        two_chunks = relu_T[:, m % 4:m % 4 + 2, :]
                        act.activation(two_chunks, two_chunks, ACT.Square).then_inc(squared, 1)
                    if (one := lagged(it, s, 1)) and (has("own", it) or (s < 1 and it == B)):
                        exps(*one)
                    if s % 4 == 3 and (got := lagged(it, s, 7)) and (has("own", it) or (s == 3 and it == B)):
                        b, h = got
                        g = h // 4
                        take_wait(act, f"pv{g}", it)
                        if not (isinstance(b, int) and b == 0 and g == 0):
                            pb, pg = (b, g - 1) if g else (b - 1, 3)
                            take_wait(act, f"otok{pg}", pb + 1 if pg >= 2 else pb)
                        k = BANK_OF[f"pv{g}"]
                        act.activation(oT[:, 0:S], bank[k][:, 0:S], ACT.Copy).then_inc(drained[k], 1)
                    if s == 0 and has("next", it):
                        act.wait_ge(edges_ready, nxt + 1)
                        act.activation(edges[:, :, :, :], edges[:, :, :, :], ACT.Abs).then_inc(edges_abs, 1)
                    if s in ONT_SLOTS and has("prev", it):
                        c = ONT_SLOTS[s]
                        take_high(f"ont{c}", it, o_normT[0][:, c, :], o_normT_high)
                    if s == 5 and has("next", it):
                        for c in range(NC):
                            take_high(f"xt{c}", it, xT[0][:, c, :], xT_high)
                    if s == 9 and has("prev", it):
                        for c in range(NC):
                            take_high(f"x2t{c}", it, x2T[0][:, c, :], x2T_high)
                    if has("next", it):
                        for j in QK_SLOTS.get(s, ()):
                            take(f"qk{j}", it, qk[:, j, :], func=ACT.Identity, bias=bqk_sb[:, j:j + 1],
                                 scale=qscale_sb[:, j:j + 1] if j < NC else 1.0)
                    if s in FFN_SLOTS and has("prev", it):
                        m = FFN_SLOTS[s][0]
                        if not (isinstance(it, int) and it == 1 and m < 4):
                            act.wait_ge(squares_ready, (it - 1) * 4 + m // 2 - 1)
                        take(f"ffn{m}", it, relu_T[:, m % 4, :], func=ACT.Relu)
                    if turning:
                        take_turned(b2, h2, 2)

            act.wait_ge(bias_scaled, 1)
            iterations(act, body)

        @block.vector
        def _(dve):
            steps = [0]

            def step(ins):
                steps[0] += 1
                ins.then_inc(dve_step, 1)
                dve.wait_ge(dve_step, steps[0])

            dve.wait_ge(pool_step, 1)
            step(dve.tensor_copy(dist_f, dist_i))
            step(dve.tensor_scalar(dist[:, :], dist_f, -1.0, None, ALU.mult))
            step(dve.tensor_tensor(dist[:, :], dist_f, dist[:, :], ALU.min))

            def split(parts, src, where):
                step(dve.tensor_copy(parts[0][where], src))
                return dve.tensor_tensor(parts[1][where], src, parts[0][where].bitcast(F32), ALU.subtract)

            dve.wait_ge(qkv_loaded, 16 * 7)
            dve.tensor_tensor(bqk_sb[:, 0:NC], bqk_sb[:, 0:NC], qscale_sb[:, :], ALU.mult).then_inc(bias_scaled, 1)
            everything = (slice(None), slice(None), slice(None))
            step(split(wqkv, wqkv_raw, everything))
            step(split(wo, wo_raw, everything))
            dve.wait_ge(rows_ready, 2)

            def ternary_scale(w, width, scale, half):
                step(dve.tensor_reduce(scale[:, :], w, AX.X, ALU.add, apply_absolute_value=True))
                step(dve.tensor_scalar(scale[:, :], scale[:, :], 1.0 / width, 1e-5, ALU.mult, ALU.max))
                dve.tensor_scalar(half[:, 0, :], scale[:, :], 0.5, None, ALU.mult)
                step(dve.tensor_scalar(half[:, 1, :], scale[:, :], -0.5, None, ALU.mult))

            def ternary_sign(dst, tmp, w, half, i):
                step(dve.tensor_scalar(tmp, w[:, i, :], half[:, 1, i:i + 1], None, ALU.is_lt))
                return dve.scalar_tensor_tensor(out=dst, in0=w[:, i, :], scalar=half[:, 0, i:i + 1], in1=tmp,
                                                op0=ALU.is_gt, op1=ALU.subtract)

            def ternary_fc(s):
                if s == 6:
                    dve.wait_ge(ffn_loaded, 16 * 6)
                    ternary_scale(w1_nat[:, :, :], D, scale1, half1)
                for m in {6: (0, 1), 11: (2, 3), 12: (4, 5, 6, 7)}.get(s, ()):
                    tern = ternary[:, (m % 4) * D:(m % 4 + 1) * D]
                    step(ternary_sign(tern, tern, w1_nat, half1, m))
                    step(dve.tensor_tensor(tern, tern, w1_nat[:, m, :], ALU.subtract))
                    step(dve.tensor_tensor(w1_nat[:, m, :], w1_nat[:, m, :], tern, ALU.add))

            def prepare_fc(s):
                if s == 0:
                    take("low_bv", 0, lambda ps: dve.tensor_scalar(low_bv[:, :], ps[0:RANK, 0:D], gate_bc[0:RANK, :],
                                                                   None, ALU.mult))
                if 1 <= s <= NM // 2:
                    for m in (2 * s - 2, 2 * s - 1):
                        name = f"low{m - m % 2}{m - m % 2 + 1}"
                        take_wait(dve, name, 0)
                        last = dve.scalar_tensor_tensor(
                            out=w1_nat[:, m, :], in0=w1_nat[:, m, :], scalar=scale1[:, m:m + 1],
                            in1=bank[BANK_OF[name]][:, (m % 2) * D:(m % 2 + 1) * D], op0=ALU.mult, op1=ALU.add)
                        if m % 2:
                            last.then_inc(drained[BANK_OF[name]], 1)
                if 6 <= s <= 9:
                    n = s - 6
                    m = 4 * (n % 2)
                    take(f"w1t{n}", 0, lambda ps: split(
                        w1T, ps[:, :], (slice(None), n // 2, slice(m * P, (m + 4) * P))))

            def prepare_proj(s):
                if s == 10:
                    ternary_scale(w2_nat[:, :, :], HID, scale2, half2)
                    for c in range(NC):
                        last = dve.tensor_copy(scale2_cols[:, c, :], scale2[:, c:c + 1].to_broadcast([P, P]))
                    last.then_inc(scale2_ready, 1)
                if s in (12, 13):
                    step(ternary_sign(w2_nat[:, s - 12, :], ternary, w2_nat, half2, s - 12))
                if s == 13:
                    dve.sem_inc(w2_ready, 1)
                if s in (14, 15):
                    for n in (2 * (s - 14), 2 * (s - 14) + 1):
                        take(f"w2t{n}", 0, lambda ps: dve.tensor_copy(
                            w2T[:, 2 * n:2 * n + 2, :].rearrange("p m d -> p (m d)"), ps[:, :]))
                if s == 11:
                    take("scale2", 0, lambda ps: dve.tensor_copy(scale2_bc[:, :], ps[:, 0:D]))

            def take(name, it, fn):
                take_wait(dve, name, it)
                k = BANK_OF[name]
                fn(bank[k]).then_inc(drained[k], 1)

            def take_low(name, it, parts, c, high, n):
                take_wait(dve, name, it)
                wait_alone(dve, high, n)
                k = BANK_OF[name]
                dve.tensor_tensor(parts[1][:, c, :], bank[k][:, 0:SP3], parts[0][:, c, :].bitcast(F32),
                                  ALU.subtract).then_inc(drained[k], 1)

            def bias_and_max(b, h, tiles):
                for t in tiles:
                    wait_alone(dve, scores_ready, b * (NT * H) + NT * h + t + 1)
                    if t == 0 and not (isinstance(b, int) and b == 0 and h < 2):
                        wait_alone(dve, probs_ready, b * (NT * H) + NT * (h - 1))
                    dve.tensor_tensor_reduce(nscore[0:rows(t), h % 2, t, :],
                                             score_ps[t][0:rows(t), 0:S],
                                             dist[0:rows(t), (2 - t) * P:(2 - t) * P + S],
                                             -slope(h), 3.0e38, ALU.add, ALU.min,
                                             nmax[0:rows(t), h % 2, t:t + 1]).then_inc(scores_taken, 1)

            def layer_norm(k, src, n):
                for t in range(NT):
                    last = dve.bn_stats(stats[:, k, t, :], src[:, t, :])
                last.then_inc(stats_done[k], 1)
                wait_alone(dve, stats_done[k], n + 1)
                for t in range(NT):
                    last = dve.bn_aggr(moments[:, k, t, :], stats[:, k, t, :])
                last.then_inc(moments_done[k], 1)

            def normalize(k, dst, src, n, ready):
                dve.wait_ge(rstd_ready[k], n + 1)
                dve.wait_ge(moments_done[k], n + 1)
                for t in range(NT):
                    last = dve.tensor_scalar(dst[:, t, :], src[:, t, :], moments[:, k, t, 0:1],
                                             rstd[:, k, t:t + 1], ALU.subtract, ALU.mult)
                last.then_inc(ready, 1)

            def take_v(name, it, t, n):
                take(name, it, lambda ps: dve.tensor_tensor(
                    v_sb[:, t:t + n, :, 0:HD],
                    ps[:, 0:n * D].rearrange("p (t h c) -> p t h c", t=n, h=H),
                    bias_bc[:, 0, :].rearrange("p (t h c) -> p t h c", t=1, h=H).to_broadcast([P, n, H, HD]),
                    ALU.add))

            def head_outputs(b, g, it):
                name = f"otok{g}"
                take_wait(dve, name, it)
                k = BANK_OF[name]
                ps = bank[k][:, 0:SP3].rearrange("p (t j c) -> p t j c", t=NT, j=4)
                dve.reciprocal(recip[:, :, :], ps[:, :, :, HD]).then_inc(recip_ready, 1)
                dve.wait_ge(recip_ready, b * 4 + g + 1)
                dve.tensor_tensor(o_norm[:, :, 64 * g:64 * g + 64].rearrange("p t (j c) -> p t j c", j=4),
                                  ps[:, :, :, 0:HD],
                                  recip[:, :, :].rearrange("p t (j c) -> p t j c", c=1).to_broadcast([P, NT, 4, HD]),
                                  ALU.mult).then_inc(drained[k], 1)

            def body(it):
                nxt, prv = it + 1, it - 1
                for s in range(H):
                    if has("own", it):
                        bias_and_max(it, s, (0, 1))
                    if (two := lagged(it, s, 2)) and (has("own", it) or (s < 2 and it == B)):
                        b, h = two
                        ring_wait(dve, it, s)
                        k, n = turn(b, h, 1)
                        dve.wait_ge(turned[k], n)
                        dve.tensor_copy(probsT[0:rows(1), h % RING, 1, :],
                                        turn_ps[k][0:rows(1), 0:S]).then_inc(turned_taken[k], 1)
                    if has("own", it):
                        bias_and_max(it, s, (2,))
                    if s == 0 and has("prev", it):
                        head_outputs(prv, 2, it)
                    if s == 2 and has("next", it):
                        dve.wait_ge(tokens_ready, nxt + 1)
                        layer_norm(0, h_new, nxt)
                    if s == 3 and has("next", it):
                        normalize(0, xn, h_new, nxt, xn_ready)
                    if s == 4:
                        if has("prev", it):
                            head_outputs(prv, 3, it)
                        if has("own", it):
                            take_v("v01", it, 0, 2)
                    if s == 5 and has("own", it):
                        take_v("v2", it, 2, 1)
                    if s in ONT_SLOTS and has("prev", it):
                        c = ONT_SLOTS[s]
                        take_low(f"ont{c}", it, o_normT, c, o_normT_high, prv * NC + c + 1)
                    if s == 5 and has("next", it):
                        for c in range(NC):
                            take_low(f"xt{c}", it, xT, c, xT_high, nxt * NC + c + 1)
                    if s == 9 and has("prev", it):
                        for c in range(NC):
                            take_low(f"x2t{c}", it, x2T, c, x2T_high, prv * NC + c + 1)
                    if s == 10 and has("own", it):
                        head_outputs(it, 0, it)
                    if s == 6 and has("prev", it):
                        dve.wait_ge(h_old_loaded, it * 16)
                        if has("late", it):
                            dve.wait_ge(y_summed, it - 1)
                        take("proj0", it, lambda ps: dve.tensor_tensor(
                            h_mid[:, 0:2, :].rearrange("p t d -> p (t d)"), ps[:, :],
                            h_old[:, 0:2, :].rearrange("p t d -> p (t d)"), ALU.add))
                        take("proj1", it, lambda ps: dve.tensor_tensor(h_mid[:, 2, :], ps[:, 0:D],
                                                                       h_old[:, 2, :], ALU.add))
                    if s == 7 and has("prev", it):
                        step_taken(dve, "proj1", it)
                        layer_norm(1, h_mid, prv)
                    if s == 8 and has("prev", it):
                        dve.wait_ge(stored, it * 32)
                        normalize(1, x2, h_mid, prv, x2_ready)
                    if s == 11:
                        if has("next", it):
                            for j in range(NQ):
                                step_taken(dve, f"qk{j}", it)
                            dve.tensor_copy(qk_parts[:, 0, :, :], qk[:, :, :]).then_inc(high_ready, 1)
                    if s == 12 and has("own", it):
                        head_outputs(it, 1, it)
                    if s in FFN_SLOTS and has("prev", it):
                        m = FFN_SLOTS[s][1]
                        if not (isinstance(it, int) and it == 1 and m < 4):
                            dve.wait_ge(squares_ready, (it - 1) * 4 + m // 2 - 1)
                        take(f"ffn{m}", it, lambda ps: dve.tensor_scalar(relu_T[:, m % 4, :], ps[:, 0:S], 0.0, None,
                                                                         ALU.max))
                    if s in SQUARE_SLOTS and has("prev", it):
                        m = SQUARE_SLOTS[s]
                        dve.wait_ge(squared, prv * 4 + m // 2 + 1)
                        dve.tensor_copy(act_T[0][:, m:m + 2, :], relu_T[:, m % 4:m % 4 + 2, :]).then_inc(
                            square_high, 1)
                    if s == 12 and has("next", it):
                        dve.wait_ge(rest_ready, nxt + 1)
                        dve.tensor_copy(qk_parts[:, 1, :, :], qk[:, :, :]).then_inc(middle_ready, 1)
                    if s in Y_SLOTS and has("late", it):
                        t = Y_SLOTS[s]
                        take(f"y{t}", it, lambda ps: dve.tensor_tensor(
                            y_sb[0:rows(t), t, :], ps[0:rows(t), 0:D], scale2_bc[0:rows(t), :], ALU.mult))
                    if isinstance(it, int) and it == -1:
                        ternary_fc(s)
                    if has("weights", it):
                        prepare_fc(s)
                        prepare_proj(s)

            iterations(dve, body)

        @block.tensor
        def _(pe):
            pe.wait_ge(consts_ready, 2)

            def prepare_fc(s):
                if s == 0:
                    pe.wait_ge(ffn_loaded, 16 * 6)
                    fill("low_bv", 0, lambda ps: pe.matmul(ps[0:RANK, 0:D], low_bT, low_v, start=True, stop=True))
                if 1 <= s <= NM // 2:
                    if s == 1:
                        step_taken(pe, "low_bv", 0)

                    def low_rank(ps, m):
                        for i in range(2):
                            last = pe.matmul(ps[:, i * D:(i + 1) * D],
                                             low_uT[m // 4][:, ((m + i) % 4) * P:((m + i) % 4 + 1) * P], low_bv[:, :],
                                             start=True, stop=True)
                        return last
                    fill(f"low{2 * s - 2}{2 * s - 1}", 0, lambda ps: low_rank(ps, 2 * s - 2))
                if 6 <= s <= 9:
                    if s == 6:
                        for m in range(0, NM, 2):
                            step_taken(pe, f"low{m}{m + 1}", 0)
                    n = s - 6
                    fill(f"w1t{n}", 0, lambda ps: transpose_four(
                        ps, [w1_nat[:, 4 * (n % 2) + i, (n // 2) * P:(n // 2 + 1) * P] for i in range(4)]))

            def prepare_proj(s):
                if s in (14, 15):
                    pe.wait_ge(w2_ready, 1)
                    for n in (2 * (s - 14), 2 * (s - 14) + 1):
                        fill(f"w2t{n}", 0, lambda ps: transpose_four(
                            ps, [w2_nat[:, c, m * P:(m + 1) * P] for m in (2 * n, 2 * n + 1) for c in range(NC)]))
                if s == 11:
                    pe.wait_ge(scale2_ready, 1)

                    def scale_row(ps):
                        for c in range(NC):
                            last = pe.matmul(ps[:, c * P:(c + 1) * P], scale2_cols[:, c, :], ident[:, :], start=True,
                                             stop=True)
                        return last
                    fill("scale2", 0, scale_row)

            def transpose_four(ps, blocks):
                for i, src in enumerate(blocks):
                    last = pe.transpose(ps[:, i * P:(i + 1) * P], src, ident[:, :])
                return last

            def scores(b, h):
                for half in range(2):
                    if h == HALF * half:
                        pe.wait_ge(aug_loaded[half], b * 192 + 192)
                for t in range(NT):
                    n = NT * h + t
                    if not (isinstance(b, int) and b == 0 and h == 0):
                        pe.wait_ge(scores_taken, b * (NT * H) + n - 2)
                    pe.matmul(score_ps[t][0:rows(t), 0:S], q_aug[:, h, t * P:t * P + rows(t)], k_aug[:, h, :],
                              start=True, stop=True).then_inc(scores_ready, 1)

            def transpose_probs(b, h, tiles):
                pe.wait_ge(probs_ready, b * (NT * H) + NT * (h + 1))
                for u in tiles:
                    k, n = turn(b, h, u)
                    if not (isinstance(b, int) and b == 0 and NT * h + u < 2):
                        pe.wait_ge(turned_taken[k], n - 1)
                    for t in range(NT):
                        last = pe.transpose(turn_ps[k][0:rows(u), t * P:t * P + rows(t)],
                                            probs[0:rows(t), h % 2, t, u * P:u * P + rows(u)],
                                            ident[0:rows(t), 0:rows(t)])
                    last.then_inc(turned[k], 1)

            def times_v(b, g, it):
                for k in range(2):
                    pe.wait_ge(turned_taken[k], b * (NT * H // 2) + 6 * (g + 1))
                name = f"pv{g}"
                if g == 0:
                    for v_name in ("v01", "v2"):
                        step_taken(pe, v_name, it)
                fill_wait(pe, name, it)
                k = BANK_OF[name]
                for u in range(NT):
                    for j in range(4):
                        h = 4 * g + j
                        last = pe.matmul(bank[k][32 * j:32 * j + 32, 0:S], v_sb[0:rows(u), u, h, :],
                                         probsT[0:rows(u), h % RING, u, :], start=(u == 0), stop=(u == NT - 1))
                last.then_inc(filled[k], 1)

            def fill(name, it, fn):
                fill_wait(pe, name, it)
                k = BANK_OF[name]
                fn(bank[k]).then_inc(filled[k], 1)

            def transpose_rows(src, c):
                def fn(ps):
                    for t in range(NT):
                        last = pe.transpose(ps[:, t * P:(t + 1) * P], src[:, t, c * P:(c + 1) * P], ident[:, :])
                    return last
                return fn

            def split_product(dst, lhs, rhs, n=NC, products=((0, 0), (0, 1), (1, 0))):
                for c in range(n):
                    for a, b in products:
                        last = pe.matmul(dst, lhs(a, c), rhs(b, c), start=(c == 0 and (a, b) == products[0]),
                                         stop=(c == n - 1 and (a, b) == products[-1]))
                return last

            def head_outputs(b, g, it):
                step_taken(pe, f"pv{g}", it, back=int(g == 2))

                def fn(ps):
                    for t in range(NT):
                        last = pe.transpose(ps[:, t * P:(t + 1) * P], oT[:, t * P:(t + 1) * P], ident[:, :])
                    return last
                fill(f"otok{g}", it, fn)

            def v_rows(ps, tiles):
                for i, t in enumerate(tiles):
                    last = split_product(ps[:, i * D:(i + 1) * D],
                                         lambda a, c: xT[a][:, c, t * P:(t + 1) * P],
                                         lambda b, c: wqkv[b][:, c, 2 * D:3 * D])
                return last

            def body(it):
                nxt, prv = it + 1, it - 1
                for s in range(H):
                    if has("own", it):
                        scores(it, s)
                    two = lagged(it, s, 2)
                    turning = two and (has("own", it) or (s < 2 and it == B))
                    if turning:
                        transpose_probs(*two, (0, 1))
                    if s % 4 == 3 and (got := lagged(it, s, 7)) and (has("own", it) or (s == 3 and it == B)):
                        times_v(got[0], got[1] // 4, it)
                    if s == 0 and has("prev", it):
                        head_outputs(prv, 2, it)
                    if s == 5 and has("own", it):
                        fill("v2", it, lambda ps: v_rows(ps, (2,)))
                    if s in ONT_SLOTS and has("prev", it):
                        c = ONT_SLOTS[s]
                        step_taken(pe, "otok3" if c else "otok2", it)
                        fill(f"ont{c}", it, transpose_rows(o_norm, c))
                    if s in Y_SLOTS and has("late", it):
                        t = Y_SLOTS[s]
                        pe.wait_ge(squares_ready, (it - 1) * (NM // 2))
                        fill(f"y{t}", it, lambda ps: split_product(
                            ps[0:rows(t), 0:D], lambda a, m: act_T[a][:, m, t * P:t * P + rows(t)],
                            lambda b, m: w2T[:, m, :], n=NM, products=((0, 0), (1, 0))))
                    if s == 4:
                        if has("prev", it):
                            head_outputs(prv, 3, it)
                        if has("own", it):
                            fill("v01", it, lambda ps: v_rows(ps, (0, 1)))
                    if s == 5:
                        if has("next", it):
                            pe.wait_ge(xn_ready, nxt + 1)
                            for c in range(NC):
                                fill(f"xt{c}", it, transpose_rows(xn, c))
                    if s == 9 and has("prev", it):
                        pe.wait_ge(x2_ready, it)
                        for c in range(NC):
                            fill(f"x2t{c}", it, transpose_rows(x2, c))
                    if has("next", it):
                        for j in QK_SLOTS.get(s, ()):
                            if j == 0:
                                for c in range(NC):
                                    step_taken(pe, f"xt{c}", it)
                            fill(f"qk{j}", it, lambda ps: split_product(
                                ps[:, 0:SE], lambda a, c: wqkv[a][:, c, j * P:(j + 1) * P],
                                lambda b, c: xT[b][:, c, 0:SE]))
                    if s == 10 and has("own", it):
                        head_outputs(it, 0, it)
                    if s == 6 and has("prev", it):
                        for c in range(NC):
                            step_taken(pe, f"ont{c}", it)

                        def proj(ps, tiles):
                            for i, t in enumerate(tiles):
                                last = split_product(ps[:, i * D:(i + 1) * D],
                                                     lambda a, c: o_normT[a][:, c, t * P:(t + 1) * P],
                                                     lambda b, c: wo[b][:, c, :])
                            return last
                        fill("proj0", it, lambda ps: proj(ps, (0, 1)))
                        fill("proj1", it, lambda ps: proj(ps, (2,)))
                    if s == 12 and has("own", it):
                        head_outputs(it, 1, it)
                    if s in FFN_SLOTS and has("prev", it):
                        if s == min(FFN_SLOTS):
                            for c in range(NC):
                                step_taken(pe, f"x2t{c}", it)
                        for m in FFN_SLOTS[s]:
                            fill(f"ffn{m}", it, lambda ps: split_product(
                                ps[:, 0:SE], lambda a, c: w1T[a][:, c, m * P:(m + 1) * P],
                                lambda b, c: x2T[b][:, c, 0:SE]))
                    if has("weights", it):
                        prepare_fc(s)
                        prepare_proj(s)
                    if turning:
                        transpose_probs(*two, (2,))

            iterations(pe, body)


def kernel(**inputs):
    import concourse.bacc as bacc
    from concourse.bass_utils import run_bass_kernel_spmd

    a = {n: np.asarray(v) for n, v in inputs.items()}
    order = np.arange(2 * D).reshape(NQ, HALF, HD).transpose(0, 2, 1).reshape(-1)
    order = np.concatenate([order, np.arange(2 * D, 3 * D)])
    arrays = {
        "x_dram": a["x"],
        "txt_dram": a["txt"],
        "wqkvT_dram": np.ascontiguousarray(a["L0_attn_W_qkv"][order].T),
        "bqk_dram": np.ascontiguousarray(a["L0_attn_b_qkv"][order[:2 * D]].reshape(NQ, P).T),
        "q_scale_dram": np.array([[HD ** -0.5 / 2.0 ** (-8.0 * (HALF * j + p % HALF) / H) for j in range(NC)]
                                  for p in range(P)], np.float32),
        "bv_dram": np.ascontiguousarray(a["L0_attn_b_qkv"][2 * D:].reshape(1, D)),
        "woT_dram": np.ascontiguousarray(a["L0_attn_W_out"].T),
        "bo_dram": np.ascontiguousarray(a["L0_attn_b_out"].reshape(1, D)),
        "fast_bT_dram": np.ascontiguousarray(a["L0_ffn_fast_b"].T),
        "w_fc_dram": a["L0_ffn_w_fc"],
        "w_proj_dram": a["L0_ffn_w_proj"],
        "uT_dram": np.ascontiguousarray(a["L0_ffn_u"].T),
        "v_dram": a["L0_ffn_v"],
        "gate_dram": np.ascontiguousarray(a["L0_ffn_gate"].reshape(1, 1)),
    }
    nc = bacc.Bacc("TRN2", target_bir_lowering=False, num_devices=1)
    args = [nc.dram_tensor(n, v.shape, mybir.dt.from_np(v.dtype), kind="ExternalInput").ap()
            for n, v in arrays.items()]
    out = nc.dram_tensor("out_dram", (B, S, D), F32, kind="ExternalOutput").ap()
    early_fusion_kernel(nc, *args, out)
    return run_bass_kernel_spmd(nc, [arrays], core_ids=[0]).results[0]["out_dram"]
```
